# Optimizing a Trainium2 kernel written in Bass

```python
import numpy as np
import jax
import jax.numpy as jnp

def _softmax(x, axis=-1):
    return jax.nn.softmax(x, axis=axis)

def _gelu(x):
    return jax.nn.gelu(x, approximate=True)

def _silu(x):
    return jax.nn.silu(x)

def _sigmoid(x):
    return jax.nn.sigmoid(x)

def _layernorm(x, axis=-1, eps=1e-05):
    m = jnp.mean(x, axis=axis, keepdims=True)
    v = jnp.var(x, axis=axis, keepdims=True)
    return (x - m) / jnp.sqrt(v + eps)

def _scatter_add(tgt, idx, src, axis=0):
    return tgt.at[idx].add(src)

def _segment_sum(src, seg, n):
    return jax.ops.segment_sum(src, seg, n)
kernel_name = 'mk_recurrent_d1_jaxref_r8_9a73ae'

def setup_inputs(seed: int=0):
    np.random.seed(seed)
    _w = jnp.asarray

    def _L0_attn_setup():
        import math
        import jax, jax.numpy as jnp
        import numpy as np
        N_EMBD = 128
        N_HEAD = 16
        NUM_BUCKETS = 32
        MAX_DISTANCE = 128

        def _relative_position_bucket(relative_position, num_buckets=NUM_BUCKETS, max_distance=MAX_DISTANCE):
            rp = -jnp.minimum(relative_position, 0)
            max_exact = num_buckets // 2
            is_small = rp < max_exact
            rp_large = max_exact + (jnp.log(rp.astype(jnp.float32) / max_exact + 1e-10) / math.log(max_distance / max_exact) * (num_buckets - max_exact)).astype(jnp.int32)
            rp_large = jnp.minimum(rp_large, num_buckets - 1)
            return jnp.where(is_small, rp, rp_large)
        key = jax.random.key(seed)
        ks = jax.random.split(key, 6)
        B, T, C = (4, 256, N_EMBD)
        s_in = 1.0 / math.sqrt(C)
        x = jax.random.normal(ks[0], (B, T, C), dtype=jnp.float32)
        W_attn = jax.random.normal(ks[1], (3 * C, C), dtype=jnp.float32) * s_in
        b_attn = jnp.zeros((3 * C,), dtype=jnp.float32)
        W_proj = jax.random.normal(ks[2], (C, C), dtype=jnp.float32) * s_in
        b_proj = jnp.zeros((C,), dtype=jnp.float32)
        rel_emb = jax.random.normal(ks[3], (NUM_BUCKETS, N_HEAD), dtype=jnp.float32) * 0.02
        return {'x': x, 'W_attn': W_attn, 'b_attn': b_attn, 'W_proj': W_proj, 'b_proj': b_proj, 'rel_emb': rel_emb}
    _L0_attn_in = _L0_attn_setup()

    def _L0_ffn_setup():
        import jax, jax.numpy as jnp
        import numpy as np
        NUM_NOD = 6
        MAX_PREV = 5
        NUM_EDGE = 20
        D = 128
        H = 8
        LN_EPS = 1e-06

        def _layernorm(x, g, b):
            mu = jnp.mean(x, axis=-1, keepdims=True)
            var = jnp.mean(jnp.square(x - mu), axis=-1, keepdims=True)
            return (x - mu) * jax.lax.rsqrt(var + LN_EPS) * g + b

        def _mha(q, k, v, wq, wk, wv, wo):
            B, S, d = q.shape
            dh = d // H
            qh = (q @ wq).reshape(B, S, H, dh)
            kh = (k @ wk).reshape(B, S, H, dh)
            vh = (v @ wv).reshape(B, S, H, dh)
            scores = jnp.einsum('bqhd,bkhd->bhqk', qh, kh) / jnp.sqrt(jnp.asarray(dh, q.dtype))
            attn = jax.nn.softmax(scores, axis=-1)
            ctx = jnp.einsum('bhqk,bkhd->bqhd', attn, vh).reshape(B, S, d)
            return ctx @ wo
        key = jax.random.key(seed)
        ks = jax.random.split(key, 12)
        B, S = (8, 128)
        scale = 1.0 / np.sqrt(D)
        return {'inputs': jax.random.normal(ks[0], (B, S, D), jnp.float32), 'ew': jax.random.uniform(ks[1], (NUM_NOD, 3), jnp.float32), 'act_w': jax.random.uniform(ks[2], (NUM_NOD,), jnp.float32), 'We': jax.random.normal(ks[3], (NUM_EDGE, D, D), jnp.float32) * scale, 'be': jnp.zeros((NUM_EDGE, D), jnp.float32), 'Wq': jax.random.normal(ks[4], (NUM_NOD, D, D), jnp.float32) * scale, 'Wk': jax.random.normal(ks[5], (NUM_NOD, D, D), jnp.float32) * scale, 'Wv': jax.random.normal(ks[6], (NUM_NOD, D, D), jnp.float32) * scale, 'Wo': jax.random.normal(ks[7], (NUM_NOD, D, D), jnp.float32) * scale, 'ln_g': jnp.ones((D,), jnp.float32), 'ln_b': jnp.zeros((D,), jnp.float32)}
    _L0_ffn_in = _L0_ffn_setup()
    _d = {'L0_attn_x': _L0_attn_in['x'], 'L0_attn_W_attn': _L0_attn_in['W_attn'], 'L0_attn_b_attn': _L0_attn_in['b_attn'], 'L0_attn_W_proj': _L0_attn_in['W_proj'], 'L0_attn_b_proj': _L0_attn_in['b_proj'], 'L0_attn_rel_emb': _L0_attn_in['rel_emb'], 'L0_ffn_ew': _L0_ffn_in['ew'], 'L0_ffn_act_w': _L0_ffn_in['act_w'], 'L0_ffn_We': _L0_ffn_in['We'], 'L0_ffn_be': _L0_ffn_in['be'], 'L0_ffn_Wq': _L0_ffn_in['Wq'], 'L0_ffn_Wk': _L0_ffn_in['Wk'], 'L0_ffn_Wv': _L0_ffn_in['Wv'], 'L0_ffn_Wo': _L0_ffn_in['Wo'], 'L0_ffn_ln_g': _L0_ffn_in['ln_g'], 'L0_ffn_ln_b': _L0_ffn_in['ln_b']}
    _x0 = _d['L0_attn_x']
    _d['L0_attn_x'] = jax.random.normal(jax.random.fold_in(jax.random.key(seed), 1), (1, 2048, 128), dtype=_x0.dtype)
    del _x0
    return _d

def reference(L0_attn_x, L0_attn_W_attn, L0_attn_b_attn, L0_attn_W_proj, L0_attn_b_proj, L0_attn_rel_emb, L0_ffn_ew, L0_ffn_act_w, L0_ffn_We, L0_ffn_be, L0_ffn_Wq, L0_ffn_Wk, L0_ffn_Wv, L0_ffn_Wo, L0_ffn_ln_g, L0_ffn_ln_b):

    def _L0_attn_ref(x, W_attn, b_attn, W_proj, b_proj, rel_emb):
        import math
        import jax, jax.numpy as jnp
        import numpy as np
        N_EMBD = 128
        N_HEAD = 16
        NUM_BUCKETS = 32
        MAX_DISTANCE = 128

        def _relative_position_bucket(relative_position, num_buckets=NUM_BUCKETS, max_distance=MAX_DISTANCE):
            rp = -jnp.minimum(relative_position, 0)
            max_exact = num_buckets // 2
            is_small = rp < max_exact
            rp_large = max_exact + (jnp.log(rp.astype(jnp.float32) / max_exact + 1e-10) / math.log(max_distance / max_exact) * (num_buckets - max_exact)).astype(jnp.int32)
            rp_large = jnp.minimum(rp_large, num_buckets - 1)
            return jnp.where(is_small, rp, rp_large)
        B, T, C = x.shape
        H = N_HEAD
        D = C // H
        qkv = x @ W_attn.T + b_attn
        q, k, v = jnp.split(qkv, 3, axis=-1)
        q = q.reshape(B, T, H, D).transpose(0, 2, 1, 3)
        k = k.reshape(B, T, H, D).transpose(0, 2, 1, 3)
        v = v.reshape(B, T, H, D).transpose(0, 2, 1, 3)
        pos = jnp.arange(T)
        rel_pos = pos[None, :] - pos[:, None]
        buckets = _relative_position_bucket(rel_pos)
        rel_bias = rel_emb[buckets]
        rel_bias = rel_bias.transpose(2, 0, 1)[None]
        att = jnp.einsum('bhqd,bhkd->bhqk', q, k) * (1.0 / math.sqrt(D))
        att = att + rel_bias
        causal = jnp.tril(jnp.ones((T, T), dtype=bool))
        att = jnp.where(causal[None, None], att, -jnp.inf)
        att = jax.nn.softmax(att, axis=-1)
        y = jnp.einsum('bhqk,bhkd->bhqd', att, v)
        y = y.transpose(0, 2, 1, 3).reshape(B, T, C)
        y = y @ W_proj.T + b_proj
        return y

    def _L0_ffn_ref(inputs, ew, act_w, We, be, Wq, Wk, Wv, Wo, ln_g, ln_b):
        import jax, jax.numpy as jnp
        import numpy as np
        NUM_NOD = 6
        MAX_PREV = 5
        NUM_EDGE = 20
        D = 128
        H = 8
        LN_EPS = 1e-06

        def _layernorm(x, g, b):
            mu = jnp.mean(x, axis=-1, keepdims=True)
            var = jnp.mean(jnp.square(x - mu), axis=-1, keepdims=True)
            return (x - mu) * jax.lax.rsqrt(var + LN_EPS) * g + b

        def _mha(q, k, v, wq, wk, wv, wo):
            B, S, d = q.shape
            dh = d // H
            qh = (q @ wq).reshape(B, S, H, dh)
            kh = (k @ wk).reshape(B, S, H, dh)
            vh = (v @ wv).reshape(B, S, H, dh)
            scores = jnp.einsum('bqhd,bkhd->bhqk', qh, kh) / jnp.sqrt(jnp.asarray(dh, q.dtype))
            attn = jax.nn.softmax(scores, axis=-1)
            ctx = jnp.einsum('bhqk,bkhd->bqhd', attn, vh).reshape(B, S, d)
            return ctx @ wo
        nodes = {-1: inputs}
        lind = 0
        for c in range(NUM_NOD):
            nsrc = min(c + 1, MAX_PREV)
            snode = c - nsrc
            eq, ek, ev = (lind + nsrc - 1, lind, lind + nsrc // 2)
            in_q, in_k, in_v = (c - 1, snode, snode + nsrc // 2)
            q = ew[c, 0] * (nodes[in_q] @ We[eq] + be[eq])
            k = ew[c, 1] * (nodes[in_k] @ We[ek] + be[ek])
            v = ew[c, 2] * (nodes[in_v] @ We[ev] + be[ev])
            o = _mha(q, k, v, Wq[c], Wk[c], Wv[c], Wo[c])
            nodes[c] = act_w[c] * o + q
            lind += nsrc
        out = nodes[NUM_NOD - 1]
        return _layernorm(out, ln_g, ln_b)
    x = L0_attn_x
    xn = _layernorm(x, axis=-1)
    s = _L0_attn_ref(xn, L0_attn_W_attn, L0_attn_b_attn, L0_attn_W_proj, L0_attn_b_proj, L0_attn_rel_emb)
    g = _silu(_L0_ffn_ref(xn, L0_ffn_ew, L0_ffn_act_w, L0_ffn_We, L0_ffn_be, L0_ffn_Wq, L0_ffn_Wk, L0_ffn_Wv, L0_ffn_Wo, L0_ffn_ln_g, L0_ffn_ln_b))
    x = x + s * g
    return x

_drawn_inputs = setup_inputs


def setup_inputs(seed=0):
    import zlib

    import numpy as np

    out = dict(_drawn_inputs(seed))
    spreads = {'L0_attn_b_attn': (0.0, 0.1),
     'L0_attn_b_proj': (0.0, 0.1),
     'L0_ffn_be': (0.0, 0.1),
     'L0_ffn_ln_g': (1.0, 0.2),
     'L0_ffn_ln_b': (0.0, 0.273)}
    factors = {'L0_attn_rel_emb': 58.461, 'L0_ffn_Wq': 200.0, 'L0_ffn_Wk': 200.0}
    for name, (base, spread) in spreads.items():
        noise = np.random.default_rng([zlib.crc32(name.encode()), seed]).standard_normal(out[name].shape)
        drawn = base * np.exp(spread * noise) if base else spread * noise
        out[name] = jnp.asarray(drawn.astype(out[name].dtype))
    for name, factor in factors.items():
        out[name] = (out[name] * factor).astype(out[name].dtype)
    return out
```

```python
from contextlib import ExitStack, contextmanager
from dataclasses import dataclass, field, replace

import numpy as np

import concourse.bass as bass
from concourse import mybir

F32 = mybir.dt.float32
BF16 = mybir.dt.bfloat16
ACT = mybir.ActivationFunctionType
ALU = mybir.AluOpType
AX_X = mybir.AxisListType.X

P = 128
S = 2048
D = 128
CH = 512
NCH = S // CH
KB = S // P
TPC = CH // P
HG = 4
AH, AD = 16, 8
GH, GD = 8, 16
NODES = 6
QPARTS = (0, 0, 0, 1, 1, 2)
KPARTS = (0, 1, 2, 0, 1, 0)
AQPARTS = (0, 0, 0, 1, 1, 1, 2, 2, 2)
AKPARTS = (0, 1, 2, 0, 1, 2, 0, 1, 2)
KROWS = 96
MROWS = 3
ROWS = KROWS + MROWS
LEAD = 22
NSB = 3
NPS = 8
NEAR = 2 * P
MASKED = -1.0e30
A_SCALE = float(1.0 / np.sqrt(AD))
G_SCALE = float(1.0 / np.sqrt(GD))
LN_EPS, FFN_EPS = 1e-5, 1e-6
ASTEPS = sum(4 * (i + 1) for i in range(NCH))
GSTEPS = 2 * KB
DMA = 16
EXP_CREDIT, PV_CREDIT, MAX_CREDIT = 1, NPS, 1


@dataclass
class ExpUnit:
    n: int
    kind: str
    job: int
    kb: int
    j: int
    col: int
    near: int
    band: int
    first: bool
    last: bool
    near_n: int = -1


@dataclass
class MaxUnit:
    n: int
    kind: str
    ahead: int
    job: int
    t: int
    j: int
    k0: int
    w: int
    near: bool
    piece: int
    pieces: int
    half: int = 0


@dataclass
class Stage:
    name: str
    args: tuple
    n: int
    k: int = -1


@dataclass
class Step:
    exp: list = field(default_factory=list)
    pv: list = field(default_factory=list)
    max: list = field(default_factory=list)
    stages: list = field(default_factory=list)
    fin: object = None
    fin_n: int = -1
    loads: list = field(default_factory=list)


@dataclass
class Body:
    name: str
    kind: str
    it0: int
    n: int
    steps: list
    flags: dict
    base: dict = None
    count: dict = None


def attn_exp_units():
    steps, n = [], 0
    for i in range(NCH):
        for kb in range(4 * (i + 1)):
            r = max(kb - 4 * i, 0)
            near, band = 0, 0
            if kb >= 4 * i:
                near = min(NEAR, CH - r * P)
            elif kb == 4 * i - 1:
                near, band = P, P
            units = []
            for j in range(HG):
                units.append(ExpUnit(n, "attn", i, kb, j, r * P, near, band, kb == 0, kb == 4 * i + 3))
                n += 1
            steps.append(units)
    return steps


def graph_exp_units():
    return [[ExpUnit(4 * s + j, "graph", s // KB, s % KB, j, 0, 0, 0, s % KB == 0, s % KB == KB - 1)
             for j in range(HG)] for s in range(GSTEPS)]


def attn_max_list():
    flat = []
    for T in range(KB):
        far = max(T - 1, 0) * P
        spans = [(k, min(CH, far - k), False) for k in range(0, far, CH)]
        spans.append((far, (T + 1) * P - far, True))
        for j in range(HG):
            for p, (k0, w, near) in enumerate(spans):
                flat.append(dict(kind="attn", job=T // TPC, t=T % TPC, j=j, k0=k0, w=w, near=near,
                                 piece=p, pieces=len(spans)))
    cut = [len(flat) * p // ASTEPS for p in range(ASTEPS + 1)]
    return [flat[a:b] for a, b in zip(cut, cut[1:])]


def graph_max_list():
    return [[dict(kind="graph", job=None, t=p // HG, j=p % HG, k0=k * CH, w=CH, near=False, piece=k,
                  pieces=S // CH) for k in range(S // CH)] for p in range(KB)]


A_MAX = attn_max_list()
G_MAX = graph_max_list()
A_FIN = {i: max(p for p, u in enumerate(A_MAX) if any(x["job"] == i for x in u)) for i in range(NCH)}
MXP = max(x["pieces"] for u in A_MAX for x in u)


def attn_max_at(pos):
    ahead, p = divmod(pos, ASTEPS)
    fin = next((i for i, q in A_FIN.items() if q == p), None)
    return [dict(x, ahead=ahead, half=int(p >= LEAD)) for x in A_MAX[p]], None if fin is None else ("attn", ahead, fin)


def graph_max_at(pos):
    job, p = divmod(pos, KB)
    ahead, hg = divmod(job, 2)
    return ([dict(x, ahead=ahead, job=hg) for x in G_MAX[p]],
            ("graph", ahead, hg) if p == KB - 1 else None)


def numbered(steps):
    count = dict.fromkeys(("exp", "near", "max", "m", "misc", "M", "O", "K1", "V2", "WO", "split", "query"), 0)

    def take(what):
        count[what] += 1
        return count[what] - 1

    for st in steps:
        for u in st.exp:
            take("exp")
            if u.near:
                u.near_n = take("near")
        st.max = [MaxUnit(n=take("max"), **x) for x in st.max]
        if st.fin:
            st.fin_n = take("m")
        found = []
        for name, *args in st.stages:
            x = Stage(name, tuple(args), take("misc"))
            what = {"K2": "split", "Q2": "split", "Q1": "query"}.get(name, name)
            if what in count:
                x.k = take(what)
            found.append(x)
        st.stages = found
    return count


def body(name, kind, it0, n, steps, **flags):
    return Body(name, kind, it0, n, steps, flags, count=numbered(steps))


def lagging(units, by):
    return [replace(u, n=u.n - by) for u in units]


def attn_body(name, it0, n):
    last = it0 == AH // HG - 1
    steps = [Step(exp=units) for units in attn_exp_units()]
    for s, st in enumerate(steps):
        if s:
            st.pv = steps[s - 1].exp
            if st.pv[0].last:
                steps[s + 2].stages.append(("O", "attn", st.pv[0].job, 0))
        if last and s + LEAD >= ASTEPS:
            st.max, st.fin = graph_max_at(s + LEAD - ASTEPS)
        else:
            st.max, st.fin = attn_max_at(s + LEAD)
        if st.fin:
            steps[s + 2].stages.append(("M",) + st.fin)
    for s, x in ((1, "K1"), (4, "K2"), (8, "V1"), (10, "V2"), (16, "Q1"), (19, "Q2")):
        steps[s].stages.append((x,))
    steps[0].loads += ["attn_v", "bias_b"] + ["node_in"] + ["heads", "max_bias_a"] * (not last)
    steps[6].loads.append("split")
    steps[12].loads.append("v_out")
    if not last:
        steps[20].loads += ["bias_a", "max_bias_b"]
    steps[22].loads.append("split")
    steps.append(Step(pv=steps[-1].exp))
    steps.append(Step(stages=[("O", "attn", NCH - 1, 0)]))
    return body(name, "attn", it0, n, steps, last=last)


def graph_body(name, it0, n, after, kprep, vprep, nextq, maxes=True):
    steps = [Step(exp=units) for units in graph_exp_units()]
    for s, st in enumerate(steps):
        if s:
            st.pv = steps[s - 1].exp
        elif after:
            st.pv = lagging(steps[-1].exp, 4 * GSTEPS)
        if maxes or s + LEAD < GSTEPS:
            st.max, st.fin = graph_max_at(s + LEAD)
            if st.fin:
                steps[s + 2].stages.append(("M",) + st.fin)
    steps[0].loads += ["graph_v0", "node_in", "graph_v1"]
    if kprep:
        steps[2].stages.append(("K1",))
        steps[4].stages.append(("K2",))
        steps[5].loads.append("split")
    if after:
        for s, x in ((2, ("O", "graph", 1, -1)), (5, ("OT",)), (7, ("WO",))):
            steps[s].stages.append(x)
        steps[8].loads.append("n_out")
        if nextq:
            steps[9].stages.append(("Q1",))
            steps[14].stages.append(("Q2",))
            steps[15].loads.append("split")
    steps[18].stages.append(("O", "graph", 0, 0))
    if vprep:
        steps[17].loads.append("v_in")
        steps[20].stages.append(("V1",))
        steps[22].stages.append(("V2",))
        steps[23].loads.append("v_out")
    if it0 < NCH:
        steps[12].stages.append(("Y1",))
        steps[16].stages.append(("Y2",))
    return body(name, "graph", it0, n, steps, after=after, kprep=kprep, vprep=vprep, nextq=nextq)


def tail_body(name, it0, more):
    steps = [Step(pv=lagging(graph_exp_units()[-1], 4 * GSTEPS))]
    for x in [("O", "graph", 1, -1), ("OT",), ("WO",)] + [("Q1",), ("Q2",)] * more:
        steps.append(Step(stages=[x]))
    steps[0].loads.append("node_in")
    steps[3].loads.append("n_out")
    if more:
        steps[5].loads.append("split")
        for ch in range(NCH):
            steps.append(Step(stages=[("V1", ch), ("V2", ch)], loads=[("v_in", ch), ("v_out", ch)]))
    return body(name, "tail", it0, 1, steps, after=True, kprep=False, vprep=more, nextq=more)


def plan():
    lead = [Step() for _ in range(LEAD)]
    for p, st in enumerate(lead):
        st.max, st.fin = attn_max_at(p)
        if st.fin:
            lead[p + 2 if p + 2 < LEAD else p].stages.append(("M",) + st.fin)
    n = NCH
    bodies = [
        body("lead", "lead", 0, 1, lead),
        attn_body("attention", 0, 3),
        attn_body("attention_last", 3, 1),
        graph_body("node0_first", 0, 1, False, True, False, False),
        graph_body("node0", 1, n - 1, True, True, False, True),
        tail_body("node0_end", n, True),
        graph_body("node1_first", n, 1, False, True, True, False),
        graph_body("nodes", n + 1, (NODES - 2) * n - 1, True, True, True, True),
        graph_body("last_first", (NODES - 1) * n, 1, True, False, False, True),
        graph_body("last", (NODES - 1) * n + 1, n - 2, True, False, False, False),
        graph_body("last_end", NODES * n - 1, 1, True, False, False, False, maxes=False),
        tail_body("end", NODES * n, False),
    ]
    total = dict.fromkeys(bodies[0].count, 0)
    for b in bodies:
        b.base = dict(total)
        for k in total:
            total[k] += b.n * b.count[k]
    return bodies, total


class Iteration:

    def __init__(self, eng, v, name="", values=()):
        self.eng, self.v, self.name, self.values, self.kept = eng, v, name, values, {}

    def keep(self, name, f, multiple=1):
        if isinstance(self.v, int) or not self.values:
            return f(self.v)
        if name not in self.kept:
            reg = self.eng.alloc_register(f"{self.name}_kept{len(self.kept)}")
            self.eng.reg_mov(reg, f(self.v))
            found = [f(i) for i in self.values]
            self.kept[name] = reg, self.eng.snap(reg, donate=True, min_val=min(found), max_val=max(found),
                                                 guaranteed_mod_val=0, out_of_modulus=multiple)
        return self.kept[name][1]

    def end(self):
        for reg, _ in self.kept.values():
            self.eng.free_register(reg)


def at(b, what, local, it):
    n = b.count[what]
    if b.n == 1 or n == 0:
        return b.base[what] + local
    return it.keep(("times", n), lambda v: v * n, n) + (b.base[what] + local - b.it0 * n)


def chunk(it):
    return it % NCH


def node(it):
    return it // NCH


@contextmanager
def each(eng, b, keep=True):
    if b.n > 1:
        with eng.Fori(b.it0, b.it0 + b.n) as v:
            it = Iteration(eng, v, b.name, range(b.it0, b.it0 + b.n) if keep else ())
            yield it
            it.end()
    else:
        yield Iteration(eng, b.it0)


SETUP, STREAM = "setup", "stream"


def build(nc, x, wa, ba, ba_qk, wp, bp, rel, hot, wkv, wq, wo, be, ew, act_w, ln_g, ln_b, out):
    bodies, total = plan()
    AJOBS = (AH // HG) * NCH

    dram = lambda name, shape, dt: nc.dram_tensor(name, shape, dt, kind="Internal").ap()
    acts_d = dram("acts_d", (NODES + 1, D, S), F32)
    parts_d = dram("parts_d", (2, 3, D, S), BF16)
    split_d = dram("split_d", (3, D, CH), BF16)
    va_d = dram("va_d", (AH // HG, P, KB * HG * (AD + 1)), F32)
    vg_d = dram("vg_d", (2, 2, P, KB * HG * (GD + 1)), F32)
    line_d = dram("line_d", (AH, 2, NEAR + P), F32)
    band_d = dram("band_d", (2, AH, P, NEAR), F32)

    with ExitStack() as ctx:
        sb = lambda name, shape, dt: ctx.enter_context(nc.sbuf_tensor(name, shape, dt))
        ps = lambda name, shape, dt: ctx.enter_context(nc.psum_tensor(name, shape, dt))
        sem = lambda name: ctx.enter_context(nc.semaphore(name))

        keys = sb("keys", [P, 2 * GH * S], BF16)
        queries = sb("queries", [P, NCH * GH * CH], BF16)
        late = sb("late", [P, 2 * HG * S // 2], F32)
        probs = sb("probs", [P, NPS * CH], F32)
        vlive = sb("vlive", [P, 2, KB * HG * (GD + 1)], F32)
        bias_kq = sb("bias_kq", [P, 2, HG, NEAR], F32)
        bias_qk = sb("bias_qk", [P, 2, HG, NEAR], F32)
        w_kv = sb("w_kv", [P, 4 * D], F32)
        w_q = sb("w_q", [P, 2 * D], F32)
        eq = sb("eq", [P, NCH * CH], F32)
        xk = sb("xk", [P, CH], F32)
        edge = sb("edge", [P, CH], F32)
        whole = sb("whole", [P, CH], F32)
        rest = sb("rest", [P, CH], F32)
        parts = sb("parts", [P, 3, CH], BF16)
        o_sb = sb("o_sb", [P, 2, CH], F32)
        y_tok = sb("y_tok", [P, KB * D], F32)
        rden = sb("rden", [P, TPC, HG], F32)
        mx = sb("mx", [P, 2, TPC, HG, MXP], F32)
        neg_max = sb("neg_max", [P, HG * TPC], F32)
        neg_rest = sb("neg_rest", [P, HG * TPC], F32)
        neg_parts = sb("neg_parts", [P, MROWS, HG * TPC], BF16)
        neg_rows = sb("neg_rows", [MROWS * HG * TPC, P], BF16)
        ident = sb("ident", [P, P], F32)
        ident_b = sb("ident_b", [P, P], BF16)
        ew_all = sb("ew_all", [P, 3 * NODES], F32)
        ewb_all = sb("ewb_all", [P, 3 * NODES], F32)
        act_all = sb("act_all", [P, NODES], F32)
        ba_col = sb("ba_col", [P, 3], F32)
        stat = sb("stat", [P, 4, KB], F32)
        v_new = sb("v_new", [P, 2, TPC * HG * (GD + 1)], F32)

        aqueries = late[:].bitcast(BF16)
        s_tok = late[:, 0:S]
        n_t = late[:, S:S + CH]
        o_t = late[:, S + CH:S + 2 * CH]
        y_t = late[:, S + 2 * CH:S + 3 * CH]
        y_now = late[:, S + 3 * CH:S + 4 * CH]
        xv = late[:, S + 4 * CH:S + 5 * CH]
        o_tok = late[:, S + 5 * CH:S + 6 * CH]
        w_o = late[:, S + 6 * CH:S + 6 * CH + D]
        w_p = late[:, S + 6 * CH + D:S + 6 * CH + 2 * D]
        bp_all = late[:, S + 6 * CH + 2 * D:S + 6 * CH + 3 * D]
        x_tok = probs[:, 0:S]
        x_t = probs[:, S:2 * S]
        hot_sb = y_tok[0:32, 0:2 * (NEAR + P)]
        rel_sb = y_tok[0:32, 1000:1000 + AH]
        line_sb = y_tok[0:AH, 1024:1024 + 2 * (NEAR + P)]
        wa_sb = eq[:, 0:3 * D]
        bv_all = eq[:, 3 * D:4 * D]
        a_whole = queries[:, 0:2 * S].bitcast(F32)
        a_rest = queries[:, 2 * S:4 * S].bitcast(F32)
        a_parts = queries[:, 4 * S:7 * S]
        va_sb = keys[:, 0:2 * KB * AH * (AD + 1)].bitcast(F32)
        n_tok = queries[:, 0:2 * S].bitcast(F32)
        sq_tok = queries[:, 2 * S:4 * S].bitcast(F32)
        g_all = y_tok[:, 0:D]
        b_all = y_tok[:, D:2 * D]

        ps_s = ps("ps_s", [P, NSB, CH], F32)
        ps_m = ps("ps_m", [P, NSB, CH], F32)
        ps_o = ps("ps_o", [P, CH], F32)
        ps_x = ps("ps_x", [P, CH], F32)

        qk_done = sem("qk_done")
        bias_done = sem("bias_done")
        exp_done = sem("exp_done")
        pv_done = sem("pv_done")
        s1_done = sem("s1_done")
        max_done = sem("max_done")
        neg_done = sem("neg_done")
        neg_split = sem("neg_split")
        neg_in = sem("neg_in")
        o_done = sem("o_done")
        den_done = sem("den_done")
        misc_full = sem("misc_full")
        misc_free = sem("misc_free")
        split_done = sem("split_done")
        parts_out = sem("parts_out")
        parts_in = sem("parts_in")
        pool_chain = sem("pool_chain")
        heads_in = sem("heads_in")
        bias_kq_in = [sem(f"bias_kq{h}_in") for h in range(2)]
        bias_qk_in = [sem(f"bias_qk{h}_in") for h in range(2)]
        attn_v_in = sem("attn_v_in")
        graph_v_in = [sem("graph_v0_in"), sem("graph_v1_in")]
        v_out = sem("v_out")
        v_in = sem("v_in")
        n_out = sem("n_out")
        xk_in = sem("xk_in")
        y_in = sem("y_in")
        wkv_in = sem("wkv_in")
        wq_in = sem("wq_in")
        wo_in = sem("wo_in")
        x_in = sem("x_in")
        small_in = sem("small_in")
        hot_in = sem("hot_in")
        wa_in = sem("wa_in")
        ident_made = sem("ident_made")
        rows_made = sem("rows_made")
        zeroed = sem("zeroed")
        ewb_done = sem("ewb_done")
        ln = sem("ln")
        xt_full = sem("xt_full")
        xt_done = sem("xt_done")
        xt_out = sem("xt_out")
        line_full = sem("line_full")
        line_done = sem("line_done")
        line_out = sem("line_out")
        band_out = sem("band_out")
        proj_full = sem("proj_full")
        proj_free = sem("proj_free")
        aparts_done = sem("aparts_done")
        aparts_out = sem("aparts_out")
        va_out = sem("va_out")
        end_in = sem("end_in")
        end_full = sem("end_full")
        end_chain = sem("end_chain")
        end_out = sem("end_out")
        seen = sem("seen")

        def key_at(head, tok):
            return 2 * (head * S + tok)

        def query_at(head, tok):
            return 2 * (head * CH + tok)

        KEY_HALF, QUERY_SLOT, AQUERY_HALF = 2 * GH * S, 2 * GH * CH, 2 * HG * S
        keys_u8, queries_u8, aqueries_u8 = (x_[:].bitcast(mybir.dt.uint8) for x_ in (keys, queries, late))

        def operand(u8, rows, place, n):
            return u8[0:rows, bass.ds(place, 2 * n)].bitcast(BF16)

        def done(k):
            return k + 1

        def loaded(k, dmas=1):
            return k * (DMA * dmas) + 1

        def rows_in(jobs, kind):
            if kind in ("attn", "lead"):
                return jobs * (DMA * MROWS * HG)
            return jobs * (DMA * MROWS) + AJOBS * DMA * MROWS * (HG - 1)

        def job_of(it, u):
            if u.kind == "attn":
                return it.keep(("times", NCH), lambda v: v * NCH) + u.job
            return it.keep(("times", 2), lambda v: v * 2) + (AJOBS + u.job - (2 if u.n < 0 else 0))

        def graph_it(b, it, ahead):
            return ahead if b.kind == "attn" else it.v + ahead

        def kv_node(b, it):
            return 0 if b.kind == "attn" else node(it.v) if b.kind == "tail" else node(it.v) + 1

        def q_node(b, it):
            return 0 if b.kind == "attn" else node(it.v - 1) + 1

        def q_slot(b, it):
            return it.v if b.kind == "attn" else chunk(it.v - 1)

        def has(b, name):
            return any(x.name == name for st in b.steps for x in st.stages)

        block = ctx.enter_context(nc.Block())

        @block.tensor
        def _(pe):
            nc.tensor.sem_inc(pv_done, NPS)
            pe.wait_ge(ident_made, 2)
            pe.wait_ge(ln, 9)
            for c in range(NCH):
                bank = ps_s[:, c, :] if c < NSB else ps_m[:, 0, :]
                for t in range(TPC):
                    last = nc.tensor.transpose(bank[:, t * P:(t + 1) * P],
                                               x_tok[:, (TPC * c + t) * D:(TPC * c + t + 1) * D], ident[:])
                last.then_inc(xt_full, 1)
            pe.wait_ge(hot_in, 2 * DMA)
            for r in range(2):
                nc.tensor.matmul(ps_m[0:AH, 1 + r, 0:NEAR + P], rel_sb, hot_sb[:, r * (NEAR + P):(r + 1) * (NEAR + P)],
                                 start=True, stop=True).then_inc(line_full, 1)
            pe.wait_ge(wa_in, 2 * DMA)
            pe.wait_ge(xt_done, NCH)
            n = 0
            for r in range(2):
                for c in range(NCH):
                    if n >= NSB:
                        pe.wait_ge(proj_free, n - NSB + 1)
                    nc.tensor.matmul(ps_s[:, n % NSB, :], wa_sb[:, r * D:(r + 1) * D], x_t[:, c * CH:(c + 1) * CH],
                                     start=True, stop=True).then_inc(proj_full, 1)
                    n += 1
            for c in range(NCH):
                pe.wait_ge(proj_free, n - NSB + 1)
                for t in range(TPC):
                    last = nc.tensor.matmul(ps_s[:, n % NSB, t * D:(t + 1) * D],
                                            x_t[:, (TPC * c + t) * P:(TPC * c + t + 1) * P],
                                            wa_sb[:, 2 * D:3 * D], start=True, stop=True)
                last.then_inc(proj_full, 1)
                n += 1
            pe.wait_ge(proj_free, n)
            pe.wait_ge(line_done, 2)
            pe.wait_ge(rows_made, 5)
            pe.wait_ge(zeroed, 2)

            def scores(b, it, u):
                if u.first and u.j == 0:
                    pe.wait_ge(neg_in, rows_in(job_of(it, u) + 1, u.kind))
                pe.wait_ge(exp_done, done(at(b, "exp", u.n - NSB + 1 if u.n >= NSB else 0, it)))
                if u.kind == "attn":
                    k0 = it.keep(("heads", 0), lambda v: v % 2 * AQUERY_HALF, AQUERY_HALF)
                    q0, k0, at_byte = k0, k0 + 2 * GH * S, aqueries_u8
                    q0 = q0 + key_at(u.j, u.job * CH + u.col)
                else:
                    k0 = it.keep(("keys", 0), lambda v: node(v) % 2 * KEY_HALF, KEY_HALF)
                    q0 = it.keep(("queries", 0), lambda v: chunk(v) * QUERY_SLOT, QUERY_SLOT)
                    q0, at_byte = q0 + query_at(HG * u.job + u.j, u.col), queries_u8
                head = u.j if u.kind == "attn" else HG * u.job + u.j
                nc.tensor.matmul(ps_s[:, u.n % NSB, u.col:CH], operand(keys_u8, ROWS, k0 + key_at(head, u.kb * P), P),
                                 operand(at_byte, ROWS, q0, CH - u.col), start=True, stop=True).then_inc(qk_done, 1)

            def max_scores(b, it, u):
                if u.job == 0 and u.t == 0 and u.j == 0 and u.piece == 0:
                    if u.kind == "attn":
                        pe.wait_ge(heads_in, (it.v + u.ahead + 1) * (DMA * 2 * len(AQPARTS)))
                    else:
                        pe.wait_ge(parts_in, loaded(at(b, "split", int(has(b, "K2")), it), len(QPARTS)))
                pe.wait_ge(max_done, done(at(b, "max", u.n - NSB + 1 if u.n >= NSB else 0, it)))
                head = u.j if u.kind == "attn" else HG * u.job + u.j
                if u.kind == "attn":
                    k0 = it.keep(("heads", u.ahead), lambda v: (v + u.ahead) % 2 * AQUERY_HALF, AQUERY_HALF)
                    q0, k0, at_byte = k0 + key_at(u.j, u.job * CH + u.t * P), k0 + 2 * GH * S, aqueries_u8
                else:
                    v0 = -it.v if b.kind == "attn" else 0
                    q0 = it.keep(("queries", u.ahead), lambda v: chunk(v + v0 + u.ahead) * QUERY_SLOT, QUERY_SLOT)
                    k0 = it.keep(("keys", u.ahead), lambda v: node(v + v0 + u.ahead) % 2 * KEY_HALF, KEY_HALF)
                    q0, at_byte = q0 + query_at(head, u.t * P), queries_u8
                nc.tensor.matmul(ps_m[:, u.n % NSB, 0:u.w], operand(at_byte, KROWS, q0, P),
                                 operand(keys_u8, KROWS, k0 + key_at(head, u.k0), u.w),
                                 start=True, stop=True).then_inc(s1_done, 1)

            def pv(b, it, u):
                if u.first and u.j == 0:
                    pe.wait_ge(o_done, done(job_of(it, u)))
                    if u.kind == "attn":
                        pe.wait_ge(attn_v_in, (it.v + 1) * DMA)
                    else:
                        pe.wait_ge(graph_v_in[u.job], (it.v + 1) * DMA)
                pe.wait_ge(exp_done, done(at(b, "exp", u.n + 1, it)))
                size = (AD if u.kind == "attn" else GD) + 1
                live = 0 if u.kind == "attn" else u.job
                v0 = (u.kb * HG + u.j) * size
                nc.tensor.matmul(ps_o[32 * u.j:32 * u.j + size, u.col:CH], vlive[:, live, v0:v0 + size],
                                 probs[:, (u.n % NPS) * CH + u.col:(u.n % NPS + 1) * CH],
                                 start=u.first, stop=u.last).then_inc(pv_done, 1)

            def stage(b, it, st):
                if b.base["misc"] + st.n > 0:
                    pe.wait_ge(misc_free, at(b, "misc", st.n, it))
                if st.name == "M":
                    pe.wait_ge(neg_split, at(b, "M", st.k + 1, it))
                    nc.tensor.sem_inc(seen, 1)
                    last = nc.tensor.transpose(ps_x[0:MROWS * HG * TPC, 0:P // 2].bitcast(BF16),
                                               neg_parts[:, :, :].rearrange("p m c -> p (m c)"), ident_b[:])
                elif st.name == "O":
                    pe.wait_ge(o_done, done(at(b, "O", st.k + 1, it)))
                    slot = st.args[1] % 2
                    for t in range(TPC):
                        last = nc.tensor.transpose(ps_x[:, t * P:(t + 1) * P], o_sb[:, slot, t * P:(t + 1) * P],
                                                   ident[:])
                elif st.name in ("OT", "Y1"):
                    if st.name == "Y1":
                        pe.wait_ge(y_in, (it.v + 3) * DMA)
                    for t in range(TPC):
                        src = o_tok[:, t * D:(t + 1) * D] if st.name == "OT" else y_now[:, t * D:(t + 1) * D]
                        last = nc.tensor.transpose(ps_x[:, t * P:(t + 1) * P], src, ident[:])
                elif st.name in ("Y2", "V2"):
                    stationary, w = (y_t, w_p) if st.name == "Y2" else (edge[:], w_kv[:, 3 * D:4 * D])
                    for t in range(TPC):
                        last = nc.tensor.matmul(ps_x[:, t * D:(t + 1) * D], stationary[:, t * P:(t + 1) * P], w,
                                                start=True, stop=True)
                else:
                    if st.name == "K1":
                        pe.wait_ge(xk_in, at(b, "K1", 1, it) * DMA)
                        loads = 1 if b.kind == "attn" else at(b, "K1", 1, it) - (NCH - 1)
                        pe.wait_ge(wkv_in, loads * DMA)
                        w, moving = w_kv[:, 0:D], xk[:]
                    elif st.name == "K2":
                        w, moving = w_kv[:, D:2 * D], edge[:]
                    elif st.name == "V1":
                        if b.kind != "attn":
                            pe.wait_ge(v_in, (at(b, "V2", (st.args[0] if st.args else 0) + 1, it) - NCH) * DMA)
                        w, moving = w_kv[:, 2 * D:3 * D], (xk[:] if b.kind == "attn" else xv)
                    elif st.name == "Q1":
                        loads = 1 if b.kind == "attn" else at(b, "query", 1, it) - (NCH - 1)
                        pe.wait_ge(wq_in, loads * DMA)
                        w, moving = w_q[:, 0:D], (xk[:] if b.kind == "attn" else n_t)
                    elif st.name == "Q2":
                        w, moving = w_q[:, D:2 * D], eq[:, bass.ds(q_slot(b, it) * CH, CH)]
                    elif st.name == "WO":
                        pe.wait_ge(wo_in, at(b, "WO", 1, it) * DMA)
                        w, moving = w_o, o_t
                    last = nc.tensor.matmul(ps_x[:], w, moving, start=True, stop=True)
                last.then_inc(misc_full, 1)

            for b in bodies:
                with each(pe, b) as it:
                    for st in b.steps:
                        cut = [len(st.max) * j // HG for j in range(HG + 1)]
                        for j in range(HG):
                            for u in st.exp[j:j + 1]:
                                scores(b, it, u)
                            for u in st.max[cut[j]:cut[j + 1]]:
                                max_scores(b, it, u)
                        for u in st.pv:
                            pv(b, it, u)
                        for x_ in st.stages:
                            stage(b, it, x_)

            pe.wait_ge(end_in, 4 * DMA)
            for c in range(NCH):
                bank = ps_s[:, c, :] if c < NSB else ps_m[:, 0, :]
                for t in range(TPC):
                    last = nc.tensor.transpose(bank[:, t * P:(t + 1) * P],
                                               probs[:, (TPC * c + t) * P:(TPC * c + t + 1) * P], ident[:])
                last.then_inc(end_full, 1)

        @block.scalar
        def _(act):
            nc.scalar.sem_inc(exp_done, 1)
            nc.scalar.sem_inc(o_done, 1)
            act.wait_ge(ln, 6)
            nc.scalar.activation(stat[:, 3, :], stat[:, 2, :], ACT.Sqrt).then_inc(ln, 1)
            for c in range(NCH):
                act.wait_ge(xt_full, c + 1)
                bank = ps_s[:, c, :] if c < NSB else ps_m[:, 0, :]
                nc.scalar.activation(x_t[:, c * CH:(c + 1) * CH], bank, ACT.Copy).then_inc(xt_done, 1)
            act.wait_ge(ewb_done, 2)
            for n in range(2 * NCH):
                r, c = divmod(n, NCH)
                if n == NCH:
                    act.wait_ge(aparts_done, 3)
                    act.wait_ge(aparts_out, DMA)
                act.wait_ge(proj_full, n + 1)
                for dst in (a_whole, a_parts):
                    last = nc.scalar.activation(dst[:, c * CH:(c + 1) * CH], ps_s[:, n % NSB, :], ACT.Identity,
                                                scale=(A_SCALE, 1.0)[r], bias=ba_col[:, (2, 1)[r]:(3, 2)[r]])
                last.then_inc(proj_free, 1)

            def exponentials(b, it, u):
                if u.near:
                    act.wait_ge(bias_done, done(at(b, "near", u.near_n + 1, it)))
                else:
                    act.wait_ge(qk_done, at(b, "exp", u.n + 1, it))
                act.wait_ge(pv_done, done(at(b, "exp", u.n, it)))
                nc.scalar.activation(probs[:, (u.n % NPS) * CH + u.col:(u.n % NPS + 1) * CH],
                                     ps_s[:, u.n % NSB, u.col:CH], ACT.Exp,
                                     scale=1.0 if u.kind == "attn" else G_SCALE).then_inc(exp_done, 1)

            def copy_outputs(b, it, u):
                act.wait_ge(pv_done, at(b, "exp", u.n + 1, it) + NPS)
                act.wait_ge(den_done, done(job_of(it, u)))
                nc.scalar.activation(o_sb[:, u.job % 2, :], ps_o[:], ACT.Copy).then_inc(o_done, 1)

            def stage(b, it, st):
                if st.name in ("O", "WO", "Y2"):
                    return
                if st.name in ("K2", "Q2"):
                    act.wait_ge(split_done, done(at(b, "split", st.k, it)))
                    act.wait_ge(parts_out, loaded(at(b, "split", st.k, it)))
                if st.name == "V2":
                    act.wait_ge(v_out, loaded(at(b, "V2", st.k, it)))
                if st.name == "M" and b.base["M"] + st.k > 0:
                    act.wait_ge(neg_in, rows_in(at(b, "M", st.k, it), b.kind))
                act.wait_ge(misc_full, at(b, "misc", st.n + 1, it))
                if st.name in ("K1", "V1", "Q1"):
                    e = 3 * (q_node if st.name == "Q1" else kv_node)(b, it) + "QKV".index(st.name[0])
                    dst = {"K1": edge[:], "V1": edge[:], "Q1": eq[:, bass.ds(q_slot(b, it) * CH, CH)]}[st.name]
                    last = nc.scalar.activation(dst, ps_x[:], ACT.Identity, scale=ew_all[:, bass.ds(e, 1)],
                                                bias=ewb_all[:, bass.ds(e, 1)])
                elif st.name in ("K2", "Q2"):
                    nc.scalar.activation(whole[:], ps_x[:], ACT.Copy)
                    last = nc.scalar.activation(parts[:, 0, :], ps_x[:], ACT.Copy)
                elif st.name == "V2":
                    for g in range(2):
                        dst = v_new[:, g, :].rearrange("p (t j e) -> p t j e", t=TPC, j=HG)[:, :, :, 0:GD]
                        src = ps_x[:].rearrange("p (t g j e) -> p g t j e", g=2, j=HG, e=GD)[:, g]
                        last = nc.scalar.activation(dst, src, ACT.Copy)
                elif st.name == "M":
                    last = nc.scalar.activation(neg_rows[:], ps_x[0:MROWS * HG * TPC, 0:P // 2].bitcast(BF16), ACT.Copy)
                else:
                    last = nc.scalar.activation({"OT": o_t, "Y1": y_t}[st.name], ps_x[:], ACT.Copy)
                last.then_inc(misc_free, 1)

            for b in bodies:
                with each(act, b) as it:
                    for st in b.steps:
                        for u in st.exp:
                            exponentials(b, it, u)
                        if st.pv and st.pv[-1].last:
                            copy_outputs(b, it, st.pv[-1])
                        for x_ in st.stages:
                            stage(b, it, x_)

            act.wait_ge(end_chain, 11)
            nc.scalar.activation(stat[:, 3, :], stat[:, 2, :], ACT.Sqrt).then_inc(end_chain, 1)
            act.wait_ge(end_chain, 16)
            nc.scalar.activation(sq_tok, n_tok, ACT.Exp, scale=-1.0).then_inc(end_chain, 1)

        @block.vector
        def _(dve):
            tiles = lambda ap: ap.rearrange("p (t d) -> p t d", d=D)
            per_tile = lambda ap: ap.unsqueeze(2).to_broadcast([P, KB, D])
            nc.vector.sem_inc(max_done, 1)
            nc.vector.sem_inc(bias_done, 1)
            nc.vector.sem_inc(den_done, 2)
            nc.vector.memset(aqueries[64:KROWS, :].bitcast(mybir.dt.uint32), 0).then_inc(zeroed, 1)
            nc.vector.memset(ps_o[:], 0.0).then_inc(zeroed, 1)
            dve.wait_ge(x_in, DMA)
            nc.vector.reduce_sum(stat[:, 0, :], tiles(x_tok), axis=AX_X).then_inc(ln, 1)
            dve.wait_ge(ln, 1)
            nc.vector.tensor_scalar(stat[:, 1, :], stat[:, 0, :], 1.0 / D, None, ALU.mult).then_inc(ln, 1)
            dve.wait_ge(ln, 2)
            nc.vector.tensor_tensor(tiles(x_tok), tiles(x_tok), per_tile(stat[:, 1, :]), ALU.subtract).then_inc(ln, 1)
            dve.wait_ge(ln, 3)
            nc.vector.tensor_tensor(x_t, x_tok, x_tok, ALU.mult).then_inc(ln, 1)
            dve.wait_ge(ln, 4)
            nc.vector.reduce_sum(stat[:, 0, :], tiles(x_t), axis=AX_X).then_inc(ln, 1)
            dve.wait_ge(ln, 5)
            nc.vector.tensor_scalar(stat[:, 2, :], stat[:, 0, :], 1.0 / D, LN_EPS, ALU.mult, ALU.add).then_inc(ln, 1)
            dve.wait_ge(ln, 7)
            nc.vector.reciprocal(stat[:, 0, :], stat[:, 3, :]).then_inc(ln, 1)
            dve.wait_ge(ln, 8)
            nc.vector.tensor_tensor(tiles(x_tok), tiles(x_tok), per_tile(stat[:, 0, :]), ALU.mult).then_inc(ln, 1)
            dve.wait_ge(small_in, 4 * DMA)
            nc.vector.tensor_tensor(ewb_all[:], ewb_all[:], ew_all[:], ALU.mult).then_inc(ewb_done, 1)
            nc.vector.tensor_scalar(ba_col[:, 2:3], ba_col[:, 0:1], A_SCALE, None, ALU.mult).then_inc(ewb_done, 1)
            nc.vector.memset(line_sb[:, 0:P], MASKED)
            nc.vector.memset(line_sb[:, NEAR + P + NEAR + 1:2 * (NEAR + P)], MASKED)
            dve.wait_ge(line_full, 1)
            nc.vector.tensor_copy(line_sb[:, P:NEAR + P], ps_m[0:AH, 1, P:NEAR + P]).then_inc(line_done, 1)
            dve.wait_ge(line_full, 2)
            nc.vector.tensor_copy(line_sb[:, NEAR + P:NEAR + P + NEAR + 1], ps_m[0:AH, 2, 0:NEAR + 1]).then_inc(line_done, 1)
            part = lambda n: a_parts[:, n * S:(n + 1) * S]
            for r in range(2):
                dve.wait_ge(proj_free, NCH * (r + 1))
                nc.vector.tensor_tensor(a_rest, a_whole, part(0), ALU.subtract).then_inc(aparts_done, 1)
                dve.wait_ge(aparts_done, 3 * r + 1)
                if r:
                    dve.wait_ge(aparts_out, DMA)
                nc.vector.tensor_copy(part(1), a_rest).then_inc(aparts_done, 1)
                dve.wait_ge(aparts_done, 3 * r + 2)
                nc.vector.tensor_tensor(part(2), a_rest, part(1), ALU.subtract).then_inc(aparts_done, 1)
            dve.wait_ge(rows_made, 1)
            for c in range(NCH):
                n = 2 * NCH + c
                dve.wait_ge(proj_full, n + 1)
                for g in range(AH // HG):
                    grp = lambda ap: ap.rearrange("p (k g j e) -> p g k j e", g=AH // HG, j=HG, e=AD)[:, g]
                    dst = va_sb.rearrange("p (g k j e) -> p g k j e", g=AH // HG, k=KB, j=HG)[
                        :, g, TPC * c:TPC * (c + 1), :, 0:AD]
                    bias = bv_all.rearrange("p (g j e) -> p g j e", g=AH // HG, j=HG)[:, g].unsqueeze(1).to_broadcast(
                        [P, TPC, HG, AD])
                    last = nc.vector.tensor_tensor(dst, grp(ps_s[:, n % NSB, :]), bias, ALU.add)
                last.then_inc(proj_free, 1)

            def add_bias(b, it, u):
                half = int(u.n >= 4 * (ASTEPS // 2))
                if u.j == 0:
                    dve.wait_ge(bias_kq_in[half], (it.v + 1) * DMA)
                dve.wait_ge(qk_done, at(b, "exp", u.n + 1, it))
                near = ps_s[:, u.n % NSB, u.col:u.col + u.near]
                nc.vector.tensor_tensor(near, near, bias_kq[:, half, u.j, u.band:u.band + u.near],
                                        ALU.add).then_inc(bias_done, 1)

            def maxima(b, it, u):
                if u.near and u.j == 0:
                    dve.wait_ge(bias_qk_in[u.half], (it.v + (u.ahead + 1)) * DMA)
                dve.wait_ge(s1_done, at(b, "max", u.n + 1, it))
                if u.near:
                    nc.vector.sem_inc(seen, 1)
                src, dst = ps_m[:, u.n % NSB, 0:u.w], mx[:, u.job % 2, u.t, u.j, u.piece:u.piece + 1]
                if u.near:
                    nc.vector.tensor_tensor_reduce(out=src, in0=src, in1=bias_qk[:, u.half, u.j, NEAR - u.w:NEAR],
                                                   scale=1.0, scalar=-3.0e38, op0=ALU.add, op1=ALU.max,
                                                   accum_out=dst).then_inc(max_done, 1)
                else:
                    nc.vector.reduce_max(dst, src, axis=AX_X).then_inc(max_done, 1)

            def negate(b, it, st):
                kind, _, job = st.fin
                dve.wait_ge(max_done, done(at(b, "max", st.max[-1].n + 1, it)))
                if b.base["m"] + st.fin_n > 0:
                    dve.wait_ge(neg_split, at(b, "m", st.fin_n, it))
                dst = neg_max[:].rearrange("p (j t) -> p t j", j=HG)
                if kind == "graph":
                    last = nc.vector.tensor_reduce(dst, mx[:, job % 2, :, :, 0:S // CH], op=ALU.max, axis=AX_X, negate=True)
                else:
                    for t in range(TPC):
                        n = max(x_["pieces"] for u_ in A_MAX for x_ in u_ if x_["job"] == job and x_["t"] == t)
                        last = nc.vector.tensor_reduce(dst[:, t, :], mx[:, job % 2, t, :, 0:n], op=ALU.max, axis=AX_X, negate=True)
                last.then_inc(neg_done, 1)

            def stage(b, it, st):
                if st.name not in ("O", "WO", "Y2"):
                    return
                dve.wait_ge(misc_full, at(b, "misc", st.n + 1, it))
                if st.name == "O":
                    size = AD if st.args[0] == "attn" else GD
                    o4 = ps_x[:].rearrange("p (t j e) -> p t j e", j=HG, e=32)
                    nc.vector.reciprocal(rden[:], o4[:, :, :, size]).then_inc(den_done, 1)
                    dve.wait_ge(den_done, at(b, "O", st.k + 1, it) + 2)
                    if st.args[0] == "attn":
                        dst = y_tok[:].rearrange("p (t f) -> p t f", f=D)[
                            :, TPC * st.args[1]:TPC * (st.args[1] + 1), bass.ds(it.v * (HG * AD), HG * AD)]
                    else:
                        dst = o_tok.rearrange("p (t f) -> p t f", f=D)[
                            :, :, HG * GD * st.args[1]:HG * GD * (st.args[1] + 1)]
                    last = nc.vector.tensor_tensor(dst.rearrange("p t (j e) -> p t j e", j=HG), o4[:, :, :, 0:size],
                                                   rden[:].unsqueeze(3).to_broadcast([P, TPC, HG, size]), ALU.mult)
                elif st.name == "WO":
                    dve.wait_ge(n_out, loaded(at(b, "WO", st.k, it)))
                    last = nc.vector.scalar_tensor_tensor(
                        out=n_t, in0=ps_x[:], scalar=act_all[:, bass.ds(node(it.v - 1), 1)],
                        in1=eq[:, bass.ds(chunk(it.v - 1) * CH, CH)], op0=ALU.mult, op1=ALU.add)
                else:
                    last = nc.vector.tensor_tensor(s_tok[:, bass.ds(it.v * CH, CH)].rearrange("p (t d) -> p t d", d=D),
                                                   ps_x[:].rearrange("p (t d) -> p t d", d=D),
                                                   bp_all.unsqueeze(1).to_broadcast([P, TPC, D]), ALU.add)
                last.then_inc(misc_free, 1)

            for b in bodies:
                with each(dve, b) as it:
                    for st in b.steps:
                        cut = [len(st.max) * j // HG for j in range(HG + 1)]
                        for j in range(HG):
                            for u in st.exp[j:j + 1]:
                                if u.near:
                                    add_bias(b, it, u)
                            for u in st.max[cut[j]:cut[j + 1]]:
                                maxima(b, it, u)
                        if st.fin:
                            negate(b, it, st)
                        for x_ in st.stages:
                            stage(b, it, x_)

            def link(ins, n):
                ins.then_inc(end_chain, 1)
                dve.wait_ge(end_chain, n)

            bank = lambda c: tiles(ps_s[:, c, :] if c < NSB else ps_m[:, 0, :])
            for c in range(NCH):
                dve.wait_ge(end_full, c + 1)
                last = nc.vector.reduce_sum(stat[:, 0, TPC * c:TPC * (c + 1)], bank(c), axis=AX_X)
            link(last, 1)
            link(nc.vector.tensor_scalar(stat[:, 1, :], stat[:, 0, :], 1.0 / D, None, ALU.mult), 2)
            for c in range(NCH):
                link(nc.vector.tensor_tensor(tiles(n_tok)[:, TPC * c:TPC * (c + 1), :], bank(c),
                                             stat[:, 1, TPC * c:TPC * (c + 1)].unsqueeze(2).to_broadcast([P, TPC, D]),
                                             ALU.subtract), 3 + c)
            link(nc.vector.tensor_tensor(sq_tok, n_tok, n_tok, ALU.mult), 7)
            link(nc.vector.reduce_sum(stat[:, 0, :], tiles(sq_tok), axis=AX_X), 8)
            link(nc.vector.tensor_scalar(stat[:, 2, :], stat[:, 0, :], 1.0 / D, FFN_EPS, ALU.mult, ALU.add), 9)
            nc.vector.sem_inc(end_chain, 2)
            dve.wait_ge(end_chain, 12)
            link(nc.vector.reciprocal(stat[:, 0, :], stat[:, 3, :]), 13)
            link(nc.vector.tensor_tensor(tiles(n_tok), tiles(n_tok), per_tile(stat[:, 0, :]), ALU.mult), 14)
            row = lambda ap: ap.unsqueeze(1).to_broadcast([P, KB, D])
            link(nc.vector.tensor_tensor(tiles(n_tok), tiles(n_tok), row(g_all), ALU.mult), 15)
            nc.vector.tensor_tensor(tiles(n_tok), tiles(n_tok), row(b_all), ALU.add).then_inc(end_chain, 1)
            dve.wait_ge(end_chain, 17)
            link(nc.vector.tensor_scalar(sq_tok, sq_tok, 1.0, None, ALU.add), 18)
            link(nc.vector.reciprocal(sq_tok, sq_tok), 19)
            link(nc.vector.tensor_tensor(n_tok, n_tok, sq_tok, ALU.mult), 20)
            link(nc.vector.tensor_tensor(n_tok, n_tok, s_tok, ALU.mult), 21)
            nc.vector.tensor_tensor(n_tok, n_tok, x_t, ALU.add).then_inc(end_chain, 1)

        @block.gpsimd
        def _(pool):
            nc.gpsimd.sem_inc(split_done, 1)
            for n, m in enumerate((ident, ident_b)):
                nc.gpsimd.memset(m[:], 0.0).then_inc(pool_chain, 1)
                pool.wait_ge(pool_chain, n + 1)
                nc.gpsimd.affine_select(out=m[:], in_=m[:], compare_op=ALU.not_equal, fill=1.0, base=0,
                                        pattern=[[-1, P]], channel_multiplier=1).then_inc(ident_made, 1)
            ones2 = 0x3F803F80
            half = lambda r0, r1, par: keys[r0:r1, par * GH * S:(par + 1) * GH * S].bitcast(mybir.dt.uint32)
            pool.wait_ge(ident_made, 2)
            nc.gpsimd.memset(va_sb, 1.0).then_inc(rows_made, 1)
            pool.wait_ge(rows_made, 1)
            nc.gpsimd.memset(v_new[:, :, :], 1.0).then_inc(rows_made, 1)
            pool.wait_ge(rows_made, 2)
            nc.gpsimd.memset(half(64, KROWS, 1), 0).then_inc(rows_made, 1)
            pool.wait_ge(rows_made, 3)
            nc.gpsimd.memset(half(KROWS, ROWS, 1), ones2).then_inc(rows_made, 1)
            pool.wait_ge(rows_made, 4)
            pool.wait_ge(va_out, DMA)
            nc.gpsimd.memset(half(KROWS, ROWS, 0), ones2).then_inc(rows_made, 1)

            def chain(b, it, fins, splits, k):
                return 3 * at(b, "m", fins, it) + 2 * at(b, "split", splits, it) + (k + 2)

            def split_maxima(b, it, n, splits):
                pool.wait_ge(neg_done, at(b, "m", n + 1, it))
                if b.base["m"] + n > 0:
                    pool.wait_ge(neg_in, rows_in(at(b, "m", n, it), b.kind))
                nc.gpsimd.sem_inc(seen, 1)
                nc.gpsimd.tensor_copy(neg_parts[:, 0, :], neg_max[:]).then_inc(pool_chain, 1)
                pool.wait_ge(pool_chain, chain(b, it, n, splits, 1))
                nc.gpsimd.tensor_tensor(neg_rest[:], neg_max[:], neg_parts[:, 0, :], ALU.subtract).then_inc(pool_chain, 1)
                pool.wait_ge(pool_chain, chain(b, it, n, splits, 2))
                nc.gpsimd.sem_inc(seen, 1)
                nc.gpsimd.tensor_copy(neg_parts[:, 1, :], neg_rest[:]).then_inc(pool_chain, 1)
                pool.wait_ge(pool_chain, chain(b, it, n, splits, 3))
                nc.gpsimd.tensor_tensor(neg_parts[:, 2, :], neg_rest[:], neg_parts[:, 1, :], ALU.subtract)\
                    .then_inc(neg_split, 1)

            def split(b, it, st, fins):
                pool.wait_ge(misc_free, at(b, "misc", st.n + 1, it))
                nc.gpsimd.tensor_tensor(rest[:], whole[:], parts[:, 0, :], ALU.subtract).then_inc(pool_chain, 1)
                pool.wait_ge(pool_chain, chain(b, it, fins, st.k, 1))
                nc.gpsimd.sem_inc(seen, 1)
                nc.gpsimd.tensor_copy(parts[:, 1, :], rest[:]).then_inc(pool_chain, 1)
                pool.wait_ge(pool_chain, chain(b, it, fins, st.k, 2))
                nc.gpsimd.tensor_tensor(parts[:, 2, :], rest[:], parts[:, 1, :], ALU.subtract).then_inc(split_done, 1)

            for b in bodies:
                if not any(st.fin or x_.name in ("K2", "Q2") for st in b.steps for x_ in (st.stages or [Stage("", (), 0)])):
                    continue
                with each(pool, b) as it:
                    fins = splits = 0
                    for st in b.steps:
                        if st.fin:
                            split_maxima(b, it, fins, splits)
                            fins += 1
                        for x_ in st.stages:
                            if x_.name in ("K2", "Q2"):
                                split(b, it, x_, fins)
                                splits += 1

        @block.sync
        def _(sp):
            for s in (parts_in, parts_out, v_out, n_out):
                nc.sync.sem_inc(s, 1)
            sp.dma_start(x_tok.rearrange("p (t d) -> p t d", d=D), x.rearrange("(t p) d -> p t d", p=P)).then_inc(x_in, DMA)
            sp.dma_start(hot_sb, hot).then_inc(hot_in, DMA)
            sp.dma_start(rel_sb, rel).then_inc(hot_in, DMA)
            sp.dma_start(wa_sb, wa).then_inc(wa_in, DMA)
            sp.dma_start(bv_all, ba[2 * D:3 * D].unsqueeze(0).to_broadcast([P, D])).then_inc(wa_in, DMA)
            sp.dma_start(ew_all[:], ew.unsqueeze(0).to_broadcast([P, 3 * NODES])).then_inc(small_in, DMA)
            sp.dma_start(ewb_all[:], be).then_inc(small_in, DMA)
            sp.dma_start(act_all[:], act_w.unsqueeze(0).to_broadcast([P, NODES])).then_inc(small_in, DMA)
            sp.dma_start(ba_col[:, 0:2], ba_qk).then_inc(small_in, DMA)
            sp.dma_start(w_kv[:], wkv[0]).then_inc(wkv_in, DMA)
            sp.dma_start(w_q[:], wq[0]).then_inc(wq_in, DMA)
            sp.wait_ge(xt_done, NCH)
            sp.dma_start(acts_d[0], x_t).then_inc(xt_out, DMA)
            sp.wait_ge(line_done, 2)
            sp.dma_start(line_d, line_sb.rearrange("h (r n) -> h r n", r=2)).then_inc(line_out, DMA)
            sp.wait_ge(line_out, DMA)
            line_len = NEAR + P
            for r in range(2):
                src = bass.AP(tensor=line_d.tensor, offset=r * line_len + P,
                              ap=[[2 * line_len, AH], [-1, P], [1, NEAR]])
                sp.dma_start(band_d[r], src).then_inc(band_out, DMA)
            for r in range(2):
                sp.wait_ge(aparts_done, 3 * (r + 1))
                sp.dma_start(parts_d[r].rearrange("n p s -> p n s"), a_parts.rearrange("p (n s) -> p n s", n=3))\
                    .then_inc(aparts_out, DMA)
            sp.wait_ge(proj_free, 3 * NCH)
            sp.dma_start(va_d.rearrange("g p e -> p g e"), va_sb.rearrange("p (g e) -> p g e", g=AH // HG))\
                .then_inc(va_out, DMA)
            sp.wait_ge(xt_out, DMA)
            sp.wait_ge(band_out, 2 * DMA)
            sp.wait_ge(aparts_out, 2 * DMA)
            sp.wait_ge(zeroed, 1)
            sp.wait_ge(rows_made, 4)
            keys4 = keys[:].rearrange("p (a h s) -> p a h s", a=2, h=GH)
            queries4 = queries[:].rearrange("p (c h s) -> p c h s", c=NCH, h=GH)
            aqueries4 = aqueries.rearrange("p (a h s) -> p a h s", a=2, h=HG)

            def heads(hg):
                for side, (which, dst, first) in enumerate(((AQPARTS, aqueries4, 0), (AKPARTS, keys4, 1))):
                    for t, n in enumerate(which):
                        src = parts_d[side, n, bass.ds(hg * (HG * AD), HG * AD), :].rearrange("(j d) s -> d j s", d=AD)
                        rows = slice(AD * t, AD * (t + 1))
                        if side == 0:
                            d = aqueries[rows, bass.ds((hg % 2) * (HG * S), HG * S)]
                        else:
                            d = keys[rows, bass.ds((hg % 2) * (HG * S) + GH * S, HG * S)]
                        sp.dma_start(d.rearrange("d (j s) -> d j s", j=HG), src).then_inc(heads_in, DMA)

            def bias(side, hg, half_):
                dst, s = ((bias_kq, bias_kq_in), (bias_qk, bias_qk_in))[side]
                sp.dma_start(dst[:, half_], band_d[side, bass.ds(hg * HG, HG)].rearrange("h p n -> p h n"))\
                    .then_inc(s[half_], DMA)

            heads(0)
            bias(0, 0, 0)
            bias(1, 0, 0)
            bias(1, 0, 1)

            def load(b, it, s, what, ch):
                if what == "attn_v":
                    sp.wait_ge(pv_done, at(b, "exp", 0, it) + NPS)
                    sp.dma_start(vlive[:, 0, 0:KB * HG * (AD + 1)], va_d[bass.ds(it.v, 1)].rearrange("g p e -> (g p) e"))\
                        .then_inc(attn_v_in, DMA)
                elif what in ("graph_v0", "graph_v1"):
                    g = int(what[-1])
                    lag = 4 if b.flags["after"] and g == 0 else 0
                    sp.wait_ge(pv_done, at(b, "exp", 0, it) + (NPS - lag))
                    sp.wait_ge(v_out, loaded(at(b, "V2", 0, it)))
                    sp.dma_start(vlive[:, g, :], vg_d[bass.ds(node(it.v) % 2, 1), g].rearrange("a p e -> (a p) e"))\
                        .then_inc(graph_v_in[g], DMA)
                elif what == "node_in":
                    sp.wait_ge(misc_full, at(b, "misc", 0, it))
                    if b.kind == "attn":
                        sp.dma_start(xk[:], acts_d[0, :, bass.ds(it.v * CH, CH)]).then_inc(xk_in, DMA)
                    elif b.flags["kprep"]:
                        n = node(it.v) + 1
                        sp.dma_start(xk[:], acts_d[bass.ds(n // 5, 1), :, bass.ds(chunk(it.v) * CH, CH)]
                                     .rearrange("a p s -> (a p) s")).then_inc(xk_in, DMA)
                        sp.dma_start(w_kv[:], wkv[bass.ds(n, 1)].rearrange("a p e -> (a p) e")).then_inc(wkv_in, DMA)
                    if b.kind != "attn" and b.flags["after"]:
                        sp.dma_start(w_o, wo[bass.ds(node(it.v - 1), 1)].rearrange("a p e -> (a p) e")).then_inc(wo_in, DMA)
                    if b.kind != "attn" and b.flags["nextq"]:
                        sp.dma_start(w_q[:], wq[bass.ds(node(it.v - 1) + 1, 1)].rearrange("a p e -> (a p) e"))\
                            .then_inc(wq_in, DMA)
                    if has(b, "Y1"):
                        sp.wait_ge(exp_done, done(at(b, "exp", 0, it)))
                        if b.it0 == 0:
                            sp.dma_start(w_p, wp).then_inc(y_in, DMA)
                            sp.dma_start(bp_all, bp.unsqueeze(0).to_broadcast([P, D])).then_inc(y_in, DMA)
                        sp.dma_start(y_now, y_tok[:, bass.ds(it.v * CH, CH)]).then_inc(y_in, DMA)
                elif what == "heads":
                    sp.wait_ge(exp_done, done(at(b, "exp", 0, it)))
                    heads(it.v + 1)
                elif what == "bias_b":
                    sp.wait_ge(bias_done, done(at(b, "near", 0, it)))
                    bias(0, it.v, 1)
                elif what == "bias_a":
                    used = sum(1 for st in b.steps for u in st.exp if u.near and u.n < 4 * (ASTEPS // 2))
                    sp.wait_ge(bias_done, done(at(b, "near", used, it)))
                    bias(0, it.v + 1, 0)
                elif what == "max_bias_a":
                    sp.wait_ge(max_done, done(at(b, "max", 0, it)))
                    bias(1, it.v + 1, 0)
                elif what == "max_bias_b":
                    sp.wait_ge(max_done, done(at(b, "max", b.steps[s].max[0].n, it)))
                    bias(1, it.v + 1, 1)
                elif what == "split":
                    x_ = [y for st in b.steps[:s + 1] for y in st.stages if y.name in ("K2", "Q2")][-1]
                    sp.wait_ge(split_done, done(at(b, "split", x_.k + 1, it)))
                    sp.wait_ge(parts_in, loaded(at(b, "split", x_.k, it), len(QPARTS)))
                    sp.dma_start(split_d.rearrange("n p s -> p n s"), parts[:, :, :]).then_inc(parts_out, DMA)
                    sp.wait_ge(parts_out, loaded(at(b, "split", x_.k + 1, it)))
                    sp.wait_ge(exp_done, done(at(b, "exp", 0, it)))
                    for t in range(len(QPARTS)):
                        rows = slice(GD * t, GD * (t + 1))
                        if x_.name == "K2":
                            n, c0 = kv_node(b, it) % 2, (it.v if b.kind == "attn" else chunk(it.v)) * CH
                            dst = keys4[rows, bass.ds(n, 1), :, bass.ds(c0, CH)]
                        else:
                            dst = queries4[rows, bass.ds(q_slot(b, it), 1), :, :]
                        src = split_d[(KPARTS if x_.name == "K2" else QPARTS)[t]].rearrange("(h d) s -> d h s", d=GD)
                        sp.dma_start(dst.rearrange("d a h s -> d (a h) s"), src).then_inc(parts_in, DMA)
                elif what == "v_in":
                    first = [y for st in b.steps[s:] for y in st.stages if y.name == "V1"][0]
                    if b.kind == "tail":
                        sp.wait_ge(misc_full, at(b, "misc", first.n, it))
                        src = acts_d[1, :, ch * CH:(ch + 1) * CH]
                    else:
                        sp.wait_ge(misc_full, at(b, "misc", 0, it))
                        src = acts_d[bass.ds((node(it.v) + 2) // 2, 1), :, bass.ds(chunk(it.v) * CH, CH)].rearrange(
                            "a p s -> (a p) s")
                    sp.wait_ge(n_out, loaded(at(b, "WO", int(b.flags["after"]), it)))
                    sp.dma_start(xv, src).then_inc(v_in, DMA)
                elif what == "v_out":
                    x_ = [y for st in b.steps[:s + 1] for y in st.stages if y.name == "V2"][-1]
                    sp.wait_ge(misc_free, at(b, "misc", x_.n + 1, it))
                    c0 = ch if ch is not None else it.v if b.kind == "attn" else chunk(it.v)
                    size = TPC * HG * (GD + 1)
                    dst = vg_d[bass.ds(kv_node(b, it) % 2, 1), :, :, bass.ds(c0 * size, size)]
                    sp.dma_start(dst.rearrange("a g p e -> p (a g) e"), v_new[:, :, :]).then_inc(v_out, DMA)
                elif what == "n_out":
                    x_ = [y for st in b.steps[:s + 1] for y in st.stages if y.name == "WO"][-1]
                    sp.wait_ge(misc_free, at(b, "misc", x_.n + 1, it))
                    dst = acts_d[bass.ds(node(it.v - 1) + 1, 1), :, bass.ds(chunk(it.v - 1) * CH, CH)]
                    sp.dma_start(dst.rearrange("a p s -> (a p) s"), n_t).then_inc(n_out, DMA)

            def maximum_rows(b, it, x_):
                kind, ahead, job = x_.args
                sp.wait_ge(misc_free, at(b, "misc", x_.n + 1, it))
                n = HG * TPC
                for m in range(MROWS):
                    row = slice(KROWS + m, KROWS + m + 1)
                    if kind == "attn":
                        for j in range(HG):
                            q0 = (it.v + ahead) % 2 * (HG * S) + (j * S + job * CH)
                            sp.dma_start(aqueries[row, bass.ds(q0, CH)],
                                         neg_rows[m * n + j * TPC:m * n + (j + 1) * TPC, :]).then_inc(neg_in, DMA)
                    else:
                        q0 = chunk(graph_it(b, it, ahead)) * (GH * CH) + HG * job * CH
                        sp.dma_start(queries[row, bass.ds(q0, HG * CH)], neg_rows[m * n:(m + 1) * n, :])\
                            .then_inc(neg_in, DMA)

            for b in bodies:
                with each(sp, b, keep=False) as it:
                    for s, st in enumerate(b.steps):
                        for x_ in st.stages:
                            if x_.name == "M":
                                maximum_rows(b, it, x_)
                        for what in st.loads:
                            name, ch = what if isinstance(what, tuple) else (what, None)
                            load(b, it, s, name, ch)

            sp.wait_ge(n_out, loaded(total["WO"]))
            sp.wait_ge(pv_done, total["exp"] + NPS)
            sp.dma_start(probs[:, 0:S], acts_d[NODES]).then_inc(end_in, DMA)
            sp.dma_start(x_t.rearrange("p (t d) -> p t d", d=D), x.rearrange("(t p) d -> p t d", p=P)).then_inc(end_in, DMA)
            sp.dma_start(g_all, ln_g.unsqueeze(0).to_broadcast([P, D])).then_inc(end_in, DMA)
            sp.dma_start(b_all, ln_b.unsqueeze(0).to_broadcast([P, D])).then_inc(end_in, DMA)
            sp.wait_ge(end_chain, 22)
            sp.dma_start(out.rearrange("(t p) d -> p t d", p=P), n_tok.rearrange("p (t d) -> p t d", d=D))\
                .then_inc(end_out, DMA)
            sp.wait_ge(end_out, DMA)


def bucket_one_hot():
    buckets, far = 32, 128
    exact = buckets // 2
    d = np.arange(NEAR + 1)
    log = np.log(d.astype(np.float32) / np.float32(exact) + np.float32(1e-10))
    large = exact + (log / np.float32(np.log(far / exact)) * np.float32(buckets - exact)).astype(np.int64)
    bucket = np.where(d < exact, d, np.minimum(large, buckets - 1))
    assert bucket[P] == buckets - 1
    hot = np.zeros((buckets, 2, NEAR + P), np.float32)
    for r in range(2):
        for i in range(NEAR + P):
            dist = i - P if r == 0 else NEAR - i
            if dist >= 0:
                hot[bucket[dist], r, i] += 1.0
                hot[buckets - 1, r, i] -= 1.0
    return hot.reshape(buckets, 2 * (NEAR + P))


def kernel(**inputs):
    import concourse.bacc as bacc
    from concourse.bass_utils import run_bass_kernel_spmd

    a = {k: np.asarray(v) for k, v in inputs.items()}
    q_edge, k_edge, v_edge, first = [], [], [], 0
    for c in range(NODES):
        n = min(c + 1, 5)
        q_edge.append(first + n - 1)
        k_edge.append(first)
        v_edge.append(first + n // 2)
        first += n
    we = a["L0_ffn_We"]
    side = lambda *ws: np.ascontiguousarray(np.concatenate(ws, axis=-1))
    edges = np.stack([q_edge, k_edge, v_edge], axis=1).reshape(-1)
    arrays = {
        "x": a["L0_attn_x"].reshape(S, D),
        "wa": np.ascontiguousarray(a["L0_attn_W_attn"].T),
        "ba": a["L0_attn_b_attn"],
        "ba_qk": np.ascontiguousarray(a["L0_attn_b_attn"].reshape(3, D)[:2].T),
        "wp": np.ascontiguousarray(a["L0_attn_W_proj"].T),
        "bp": a["L0_attn_b_proj"],
        "rel": a["L0_attn_rel_emb"],
        "hot": bucket_one_hot(),
        "wkv": side(we[k_edge], a["L0_ffn_Wk"], we[v_edge], a["L0_ffn_Wv"]),
        "wq": side(we[q_edge], a["L0_ffn_Wq"]),
        "wo": a["L0_ffn_Wo"],
        "be": np.ascontiguousarray(a["L0_ffn_be"][edges].T),
        "ew": a["L0_ffn_ew"].reshape(-1),
        "act_w": a["L0_ffn_act_w"],
        "ln_g": a["L0_ffn_ln_g"],
        "ln_b": a["L0_ffn_ln_b"],
    }
    nc = bacc.Bacc("TRN2", target_bir_lowering=False, num_devices=1)
    nc.disable_value_cache = True
    args = [nc.dram_tensor("in_" + k, v.shape, mybir.dt.from_np(v.dtype), kind="ExternalInput").ap()
            for k, v in arrays.items()]
    out = nc.dram_tensor("out", (S, D), F32, kind="ExternalOutput").ap()
    build(nc, *args, out)
    got = run_bass_kernel_spmd(nc, [{"in_" + k: v for k, v in arrays.items()}], core_ids=[0])
    return got.results[0]["out"].reshape(1, S, D)
```

```python
from contextlib import ExitStack, contextmanager
from dataclasses import dataclass, field, replace

import numpy as np

import concourse.bass as bass
from concourse import mybir

F32 = mybir.dt.float32
BF16 = mybir.dt.bfloat16
ACT = mybir.ActivationFunctionType
ALU = mybir.AluOpType
AX_X = mybir.AxisListType.X

P = 128
S = 2048
D = 128
CH = 512
NCH = S // CH
KB = S // P
TPC = CH // P
HG = 4
AH, AD = 16, 8
GH, GD = 8, 16
NODES = 6
QPARTS = (0, 0, 0, 1, 1, 2)
KPARTS = (0, 1, 2, 0, 1, 0)
AQPARTS = (0, 0, 0, 1, 1, 1, 2, 2, 2)
AKPARTS = (0, 1, 2, 0, 1, 2, 0, 1, 2)
KROWS = 96
MROWS = 3
ROWS = KROWS + MROWS
LEAD = 22
NSB = 3
NPS = 8
VECTOR, START = 2.5, 150
HEAD_LOADS = 6
NEAR = 2 * P
MASKED = -1.0e30
A_SCALE = float(1.0 / np.sqrt(AD))
G_SCALE = float(1.0 / np.sqrt(GD))
LN_EPS, FFN_EPS = 1e-5, 1e-6
ASTEPS = sum(4 * (i + 1) for i in range(NCH))
GSTEPS = 2 * KB
DMA = 16


@dataclass
class ExpUnit:
    n: int
    kind: str
    job: int
    kb: int
    j: int
    col: int
    near: int
    band: int
    first: bool
    last: bool
    near_n: int = -1


@dataclass
class MaxUnit:
    n: int
    kind: str
    ahead: int
    job: int
    t: int
    j: int
    k0: int
    w: int
    near: bool
    piece: int
    pieces: int
    half: int = 0


@dataclass
class Stage:
    name: str
    args: tuple
    n: int
    k: int = -1


@dataclass
class Step:
    exp: list = field(default_factory=list)
    pv: list = field(default_factory=list)
    max: list = field(default_factory=list)
    stages: list = field(default_factory=list)
    fin: object = None
    fin_n: int = -1
    ending: list = field(default_factory=list)
    loads: list = field(default_factory=list)


@dataclass
class Body:
    name: str
    kind: str
    it0: int
    n: int
    steps: list
    flags: dict
    base: dict = None
    before: list = None
    count: dict = None


def attn_exp_units():
    steps, n = [], 0
    for i in range(NCH):
        for kb in range(4 * (i + 1)):
            r = max(kb - 4 * i, 0)
            near, band = 0, 0
            if kb >= 4 * i:
                near = min(NEAR, CH - r * P)
            elif kb == 4 * i - 1:
                near, band = P, P
            units = []
            for j in range(HG):
                units.append(ExpUnit(n, "attn", i, kb, j, r * P, near, band, kb == 0, kb == 4 * i + 3))
                n += 1
            steps.append(units)
    return steps


def graph_exp_units():
    return [[ExpUnit(4 * s + j, "graph", s // KB, s % KB, j, 0, 0, 0, s % KB == 0, s % KB == KB - 1)
             for j in range(HG)] for s in range(GSTEPS)]


def attn_max_list():
    flat = []
    for T in range(KB):
        far = max(T - 1, 0) * P
        spans = [(k, min(CH, far - k), False) for k in range(0, far, CH)]
        spans.append((far, (T + 1) * P - far, True))
        for j in range(HG):
            for p, (k0, w, near) in enumerate(spans):
                flat.append(dict(kind="attn", job=T // TPC, t=T % TPC, j=j, k0=k0, w=w, near=near,
                                 piece=p, pieces=len(spans)))
    exp = attn_exp_units()
    own = lambda p: exp[(p - LEAD) % ASTEPS]
    tensor = lambda p: sum(2.06 * (CH - u.col) for u in own(p))
    vector = lambda p: sum(VECTOR * (u.near + START) for u in own(p) if u.near)

    def fill(length):
        out, n = [], 0
        for p in range(ASTEPS):
            t, v, first = tensor(p), vector(p), n
            while n < len(flat):
                t, v = t + flat[n]["w"], v + VECTOR * (flat[n]["w"] + START)
                if max(t, v) > length and n > first:
                    break
                n += 1
            out.append(flat[first:n])
        return out, n

    low, high = 0, 64 * CH
    while high - low > 1:
        mid = (low + high) // 2
        low, high = (low, mid) if fill(mid)[1] == len(flat) else (mid, high)
    return fill(high)[0]


def graph_max_list():
    return [[dict(kind="graph", job=None, t=p // HG, j=p % HG, k0=k * CH, w=CH, near=False, piece=k,
                  pieces=S // CH) for k in range(S // CH)] for p in range(KB)]


A_MAX = attn_max_list()
G_MAX = graph_max_list()
A_FIN = {i: max(p for p, u in enumerate(A_MAX) if any(x["job"] == i for x in u)) for i in range(NCH)}
MXP = max(x["pieces"] for u in A_MAX for x in u)


def attn_max_at(pos):
    ahead, p = divmod(pos, ASTEPS)
    fin = next((i for i, q in A_FIN.items() if q == p), None)
    return [dict(x, ahead=ahead, half=int(p >= LEAD)) for x in A_MAX[p]], None if fin is None else ("attn", ahead, fin)


def graph_max_at(pos):
    job, p = divmod(pos, KB)
    ahead, hg = divmod(job, 2)
    return ([dict(x, ahead=ahead, job=hg) for x in G_MAX[p]],
            ("graph", ahead, hg) if p == KB - 1 else None)


def numbered(steps):
    count = dict.fromkeys(("exp", "near", "max", "m", "misc", "M", "O", "K1", "V1", "V2", "WO", "split", "query"), 0)

    def take(what):
        count[what] += 1
        return count[what] - 1

    for st in steps:
        for u in st.exp:
            take("exp")
            if u.near:
                u.near_n = take("near")
        st.max = [MaxUnit(n=take("max"), **x) for x in st.max]
        if st.fin:
            st.fin_n = take("m")
        found = []
        for name, *args in st.stages:
            x = Stage(name, tuple(args), take("misc"))
            what = {"K2": "split", "Q2": "split", "Q1": "query"}.get(name, name)
            if what in count:
                x.k = take(what)
            found.append(x)
        st.stages = found
    return count


def body(name, kind, it0, n, steps, **flags):
    return Body(name, kind, it0, n, steps, flags, count=numbered(steps))


def lagging(units, by):
    return [replace(u, n=u.n - by) for u in units]


def put(steps, s, stage):
    while steps[s].stages:
        s += 1
    steps[s].stages.append(stage)


def attn_body(name, it0, n):
    last = it0 == AH // HG - 1
    steps = [Step(exp=units) for units in attn_exp_units()]
    for s, x in ((1, "K1"), (4, "K2"), (8, "V1"), (10, "V2"), (16, "Q1"), (19, "Q2")):
        put(steps, s, (x,))
    steps.append(Step(pv=steps[-1].exp))
    for s, st in enumerate(steps[:ASTEPS]):
        if s:
            st.pv = steps[s - 1].exp
            if st.pv[0].last:
                put(steps, s + 2, ("O", "attn", st.pv[0].job, 0))
        if last and s + LEAD >= ASTEPS:
            st.max, st.fin = graph_max_at(s + LEAD - ASTEPS)
        else:
            st.max, st.fin = attn_max_at(s + LEAD)
        if st.fin:
            put(steps, min(s + 3, ASTEPS), ("M",) + st.fin)
    steps[0].loads += ["attn_v_rest", "bias_b"] + ["node_in"] + ["max_bias_a"] * (not last)
    steps[6].loads.append("split")
    steps[12].loads.append("v_out")
    if not last:
        for part in range(HEAD_LOADS):
            steps[1 + 2 * part].loads.append(("heads", part))
        steps[20].loads += ["bias_a", "max_bias_b"]
        steps[ASTEPS - TPC + 1].loads.append("attn_v_next")
    steps[22].loads.append("split")
    steps.append(Step(stages=[("O", "attn", NCH - 1, 0)]))
    return body(name, "attn", it0, n, steps, last=last)


def graph_body(name, it0, n, after, kprep, vprep, nextq, maxes=True, tokens=False, vnext=False, vlate=False):
    steps = [Step(exp=units) for units in graph_exp_units()]
    for s, st in enumerate(steps):
        if s:
            st.pv = steps[s - 1].exp
        elif after:
            st.pv = lagging(steps[-1].exp, 4 * GSTEPS)
        if maxes or s + LEAD < GSTEPS:
            st.max, st.fin = graph_max_at(s + LEAD)
            if st.fin:
                put(steps, s + 3, ("M",) + st.fin)
    steps[0].loads += ["graph_v0", "node_in", "graph_v1"]
    o, k, q = (2, 11, 15) if vlate else (5, 1, 11)
    if kprep:
        if vlate:
            steps[8].loads.append("key_in")
        put(steps, k, ("K1",))
        put(steps, k + 2, ("K2",))
        steps[k + 3].loads.append("split")
    if after:
        for i, x in enumerate((("O", "graph", 1, -1), ("OT",), ("WO",))):
            put(steps, o + (i if vlate else 2 * i), x)
        if vlate:
            put(steps, 5, ("V1", "next"))
            put(steps, 6, ("V2", "next"))
            steps[7].loads += ["v_out", "late_v"]
        if tokens:
            put(steps, 11, ("E",))
        else:
            steps[10].loads.append("n_out")
        if nextq:
            put(steps, q, ("Q1",))
            put(steps, q + 3, ("Q2",))
            steps[q + 4].loads.append("split")
    put(steps, 18, ("O", "graph", 0, 0))
    if vprep or vnext:
        if vprep:
            steps[17].loads.append("v_in")
        put(steps, 20, ("V1",) + ("next",) * vnext)
        put(steps, 22, ("V2",) + ("next",) * vnext)
        steps[23].loads.append("v_out")
    if it0 < NCH:
        put(steps, 24, ("Y1",))
        put(steps, 26, ("Y2",))
    if not maxes:
        steps[0].loads.append("end_in")
        steps[14].ending.append(("norm", 0, NCH - 1))
        steps[18].ending.append(("root", 0, NCH - 1))
        steps[22].ending.append(("silu", 0, NCH - 1))
        steps[25].ending.append(("output", 0, NCH - 1))
        steps[31].loads.append("output")
    return body(name, "graph", it0, n, steps, after=after, kprep=kprep, vprep=vprep, nextq=nextq, tokens=tokens,
                vlate=vlate)


def tail_body(name, it0):
    steps = [Step(pv=lagging(graph_exp_units()[-1], 4 * GSTEPS))]
    for x in (("O", "graph", 1, -1), ("OT",), ("WO",), ("E",)):
        steps.append(Step(stages=[x]))
    steps[0].loads.append("node_in")
    return body(name, "tail", it0, 1, steps, after=True, kprep=False, vprep=False, nextq=False, tokens=True,
                vlate=False)


def plan():
    lead = [Step() for _ in range(LEAD)]
    for p, st in enumerate(lead):
        st.max, st.fin = attn_max_at(p)
        if st.fin:
            lead[min(p + 3, LEAD - 1)].stages.append(("M",) + st.fin)
    n = NCH
    bodies = [
        body("lead", "lead", 0, 1, lead),
        attn_body("attention", 0, 3),
        attn_body("attention_last", 3, 1),
        graph_body("node0_first", 0, 1, False, True, False, False),
        graph_body("node0", 1, n - 1, True, True, False, True, vnext=True),
        graph_body("node1_first", n, 1, True, True, True, True, vlate=True),
        graph_body("nodes", n + 1, (NODES - 2) * n - 1, True, True, True, True),
        graph_body("last_first", (NODES - 1) * n, 1, True, False, False, True),
        graph_body("last", (NODES - 1) * n + 1, n - 2, True, False, False, False, tokens=True),
        graph_body("last_end", NODES * n - 1, 1, True, False, False, False, maxes=False, tokens=True),
        tail_body("end", NODES * n),
    ]
    total, before = dict.fromkeys(bodies[0].count, 0), dict.fromkeys(bodies[0].count, 0)
    for b in bodies:
        b.base = dict(total)
        b.before = [b.count] * (b.n > 1) + [before]
        before = b.count
        for k in total:
            total[k] += b.n * b.count[k]
    return bodies, total


class Iteration:

    def __init__(self, eng, v, name="", values=()):
        self.eng, self.v, self.name, self.values, self.kept = eng, v, name, values, {}

    def keep(self, name, f, multiple=1):
        if isinstance(self.v, int) or not self.values:
            return f(self.v)
        if name not in self.kept:
            reg = self.eng.alloc_register(f"{self.name}_kept{len(self.kept)}")
            self.eng.reg_mov(reg, f(self.v))
            found = [f(i) for i in self.values]
            self.kept[name] = reg, self.eng.snap(reg, donate=True, min_val=min(found), max_val=max(found),
                                                 guaranteed_mod_val=0, out_of_modulus=multiple)
        return self.kept[name][1]

    def end(self):
        for reg, _ in self.kept.values():
            self.eng.free_register(reg)


def at(b, what, local, it):
    n = b.count[what]
    if b.n == 1 or n == 0:
        return b.base[what] + local
    return it.keep(("times", n), lambda v: v * n, n) + (b.base[what] + local - b.it0 * n)


def bank_used(b, what, n):
    if n >= NSB:
        return n - NSB + 1
    if b.base[what] == 0:
        return 0
    last = [[m for m in range(c[what]) if m % NSB == n % NSB] for c in b.before]
    return max(m[-1] - c[what] + 1 for m, c in zip(last, b.before) if m) if any(last) else 0


def chunk(it):
    return it % NCH


def node(it):
    return it // NCH


@contextmanager
def each(eng, b, keep=True):
    if b.n > 1:
        with eng.Fori(b.it0, b.it0 + b.n) as v:
            it = Iteration(eng, v, b.name, range(b.it0, b.it0 + b.n) if keep else ())
            yield it
            it.end()
    else:
        yield Iteration(eng, b.it0)


def build(nc, x, wa, ba, ba_qk, wp, bp, rel, hot, wkv, wq, wo, be, ew, act_w, ln_g, ln_b, out):
    bodies, total = plan()
    AJOBS = (AH // HG) * NCH
    A_CHUNK = TPC * HG * (AD + 1)
    V_CHUNK = TPC * HG * (GD + 1)
    STORED = (NODES - 1) * NCH
    NORM_LINKS, END_LINKS = 11, 17

    dram = lambda name, shape, dt: nc.dram_tensor(name, shape, dt, kind="Internal").ap()
    acts_d = dram("acts_d", (NODES + 1, D, S), F32)
    parts_d = dram("parts_d", (2, 3, D, S), BF16)
    split_d = dram("split_d", (3, D, CH), BF16)
    va_d = dram("va_d", (AH // HG, P, KB * HG * (AD + 1)), F32)
    vg_d = dram("vg_d", (2, 2, P, KB * HG * (GD + 1)), F32)
    line_d = dram("line_d", (AH, 2, NEAR + P), F32)
    band_d = dram("band_d", (2, AH, P, NEAR), F32)

    with ExitStack() as ctx:
        sb = lambda name, shape, dt: ctx.enter_context(nc.sbuf_tensor(name, shape, dt))
        ps = lambda name, shape, dt: ctx.enter_context(nc.psum_tensor(name, shape, dt))
        sem = lambda name: ctx.enter_context(nc.semaphore(name))

        keys = sb("keys", [P, 2 * GH * S], BF16)
        queries = sb("queries", [P, NCH * GH * CH], BF16)
        late = sb("late", [P, 2 * HG * S // 2], F32)
        probs = sb("probs", [P, NPS * CH], F32)
        vlive = sb("vlive", [P, 2, KB * HG * (GD + 1)], F32)
        bias_kq = sb("bias_kq", [P, 2, HG, NEAR], F32)
        bias_qk = sb("bias_qk", [P, 2, HG, NEAR], F32)
        w_kv = sb("w_kv", [P, 4 * D], F32)
        w_q = sb("w_q", [P, 2 * D], F32)
        eq = sb("eq", [P, NCH * CH], F32)
        xk = sb("xk", [P, CH], F32)
        edge = sb("edge", [P, CH], F32)
        whole = sb("whole", [P, CH], F32)
        rest = sb("rest", [P, CH], F32)
        parts = sb("parts", [P, 3, CH], BF16)
        o_sb = sb("o_sb", [P, 2, CH], F32)
        y_tok = sb("y_tok", [P, KB * D], F32)
        rden = sb("rden", [P, TPC, HG], F32)
        mx = sb("mx", [P, 2, TPC, HG, MXP], F32)
        neg_max = sb("neg_max", [P, HG * TPC], F32)
        neg_rest = sb("neg_rest", [P, HG * TPC], F32)
        neg_parts = sb("neg_parts", [P, MROWS, HG * TPC], BF16)
        neg_rows = sb("neg_rows", [MROWS * HG * TPC, P], BF16)
        ident = sb("ident", [P, P], F32)
        ident_b = sb("ident_b", [P, P], BF16)
        ew_all = sb("ew_all", [P, 3 * NODES], F32)
        ewb_all = sb("ewb_all", [P, 3 * NODES], F32)
        act_all = sb("act_all", [P, NODES], F32)
        ba_col = sb("ba_col", [P, 3], F32)
        stat = sb("stat", [P, 4, KB], F32)
        v_new = sb("v_new", [P, 2, TPC * HG * (GD + 1)], F32)

        aqueries = late[:].bitcast(BF16)
        s_tok = late[:, 0:S]
        n_t = late[:, S:S + CH]
        o_t = late[:, S + CH:S + 2 * CH]
        y_t = late[:, S + 2 * CH:S + 3 * CH]
        y_now = late[:, S + 3 * CH:S + 4 * CH]
        xv = late[:, S + 4 * CH:S + 5 * CH]
        o_tok = late[:, S + 5 * CH:S + 6 * CH]
        w_o = late[:, S + 6 * CH:S + 6 * CH + D]
        w_p = late[:, S + 6 * CH + D:S + 6 * CH + 2 * D]
        bp_all = late[:, S + 6 * CH + 2 * D:S + 6 * CH + 3 * D]
        x_tok = probs[:, 0:S]
        x_t = probs[:, S:2 * S]
        hot_sb = y_tok[0:32, 0:2 * (NEAR + P)]
        rel_sb = y_tok[0:32, 1000:1000 + AH]
        line_sb = y_tok[0:AH, 1024:1024 + 2 * (NEAR + P)]
        wa_sb = eq[:, 0:3 * D]
        bv_all = eq[:, 3 * D:4 * D]
        va_cols = 2 * KB * AH * (AD + 1)
        va_sb = keys[:, 0:va_cols].bitcast(F32)
        a_rest = queries[:, 2 * S:4 * S].bitcast(F32)
        a_whole = [queries[:, 0:2 * S].bitcast(F32), keys[:, va_cols:va_cols + 2 * S].bitcast(F32)]
        a_parts = [queries[:, 4 * S:7 * S], keys[:, va_cols + 2 * S:va_cols + 5 * S]]
        n_tok, sq_tok, x_end = (keys[:, 2 * S * n:2 * S * (n + 1)].bitcast(F32) for n in range(3))
        g_all = y_tok[:, 0:D]
        b_all = y_tok[:, D:2 * D]

        ps_s = ps("ps_s", [P, NSB, CH], F32)
        ps_m = ps("ps_m", [P, NSB, CH], F32)
        ps_o = ps("ps_o", [P, CH], F32)
        ps_x = ps("ps_x", [P, CH], F32)

        qk_done = sem("qk_done")
        bias_done = sem("bias_done")
        exp_done = sem("exp_done")
        pv_done = sem("pv_done")
        s1_done = sem("s1_done")
        max_done = sem("max_done")
        neg_done = sem("neg_done")
        neg_split = sem("neg_split")
        neg_in = sem("neg_in")
        o_done = sem("o_done")
        den_done = sem("den_done")
        misc_full = sem("misc_full")
        misc_free = sem("misc_free")
        split_done = sem("split_done")
        parts_out = sem("parts_out")
        parts_in = sem("parts_in")
        pool_chain = sem("pool_chain")
        heads_in = sem("heads_in")
        bias_kq_in = [sem(f"bias_kq{h}_in") for h in range(2)]
        bias_qk_in = [sem(f"bias_qk{h}_in") for h in range(2)]
        attn_v_in = sem("attn_v_in")
        attn_v_rest_in = sem("attn_v_rest_in")
        graph_v_in = [sem("graph_v0_in"), sem("graph_v1_in")]
        v_out = sem("v_out")
        late_v_in = sem("late_v_in")
        v_in = sem("v_in")
        n_out = sem("n_out")
        xk_in = sem("xk_in")
        y_in = sem("y_in")
        wkv_in = sem("wkv_in")
        wq_in = sem("wq_in")
        wo_in = sem("wo_in")
        x_in = sem("x_in")
        small_in = sem("small_in")
        hot_in = sem("hot_in")
        wa_in = sem("wa_in")
        ident_made = sem("ident_made")
        rows_made = sem("rows_made")
        zeroed = sem("zeroed")
        zeroed_bank = sem("zeroed_bank")
        ewb_done = sem("ewb_done")
        ln = sem("ln")
        xt_full = sem("xt_full")
        xt_done = sem("xt_done")
        xt_out = sem("xt_out")
        line_full = sem("line_full")
        line_done = sem("line_done")
        line_out = sem("line_out")
        band_out = sem("band_out")
        proj_full = sem("proj_full")
        proj_free = sem("proj_free")
        aparts_done = sem("aparts_done")
        aparts_out = sem("aparts_out")
        va_out = sem("va_out")
        end_in = sem("end_in")
        end_chain = sem("end_chain")
        end_out = sem("end_out")
        seen = sem("seen")

        def key_at(head, tok):
            return 2 * (head * S + tok)

        def query_at(head, tok):
            return 2 * (head * CH + tok)

        KEY_HALF, QUERY_SLOT, AQUERY_HALF = 2 * GH * S, 2 * GH * CH, 2 * HG * S
        keys_u8, queries_u8, aqueries_u8 = (x_[:].bitcast(mybir.dt.uint8) for x_ in (keys, queries, late))

        def operand(u8, rows, place, n):
            return u8[0:rows, bass.ds(place, 2 * n)].bitcast(BF16)

        def done(k):
            return k + 1

        def loaded(k, dmas=1):
            return k * (DMA * dmas) + 1

        def rows_in(jobs):
            return jobs * (DMA * MROWS)

        def job_of(it, u):
            if u.kind == "attn":
                return it.keep(("times", NCH), lambda v: v * NCH) + u.job
            return it.keep(("times", 2), lambda v: v * 2) + (AJOBS + u.job - (2 if u.n < 0 else 0))

        def graph_it(b, it, ahead):
            return ahead if b.kind == "attn" else it.v + ahead

        def kv_node(b, it, st=None):
            return 0 if b.kind == "attn" else node(it.v - 1) + 1 if st and "next" in st.args else node(it.v) + 1

        def q_node(b, it):
            return 0 if b.kind == "attn" else node(it.v - 1) + 1

        def q_slot(b, it):
            return it.v if b.kind == "attn" else chunk(it.v - 1)

        def has(b, name):
            return any(x.name == name for st in b.steps for x in st.stages)

        block = ctx.enter_context(nc.Block())

        @block.tensor
        def _(pe):
            nc.tensor.sem_inc(pv_done, NPS)
            pe.wait_ge(ident_made, 2)
            pe.wait_ge(ln, 9)
            for c in range(NCH):
                bank = ps_s[:, c, :] if c < NSB else ps_m[:, 0, :]
                for t in range(TPC):
                    last = nc.tensor.transpose(bank[:, t * P:(t + 1) * P],
                                               x_tok[:, (TPC * c + t) * D:(TPC * c + t + 1) * D], ident[:])
                last.then_inc(xt_full, 1)
            pe.wait_ge(hot_in, 2 * DMA)
            for r in range(2):
                nc.tensor.matmul(ps_m[0:AH, 1 + r, 0:NEAR + P], rel_sb, hot_sb[:, r * (NEAR + P):(r + 1) * (NEAR + P)],
                                 start=True, stop=True).then_inc(line_full, 1)
            pe.wait_ge(wa_in, 2 * DMA)
            pe.wait_ge(xt_done, NCH)
            n = 0
            for r in range(2):
                for c in range(NCH):
                    if n >= NSB:
                        pe.wait_ge(proj_free, n - NSB + 1)
                    nc.tensor.matmul(ps_s[:, n % NSB, :], wa_sb[:, r * D:(r + 1) * D], x_t[:, c * CH:(c + 1) * CH],
                                     start=True, stop=True).then_inc(proj_full, 1)
                    n += 1
            for c in range(NCH):
                pe.wait_ge(proj_free, n - NSB + 1)
                for t in range(TPC):
                    last = nc.tensor.matmul(ps_s[:, n % NSB, t * D:(t + 1) * D],
                                            x_t[:, (TPC * c + t) * P:(TPC * c + t + 1) * P],
                                            wa_sb[:, 2 * D:3 * D], start=True, stop=True)
                last.then_inc(proj_full, 1)
                n += 1
            pe.wait_ge(proj_free, n)
            pe.wait_ge(line_done, 2)
            pe.wait_ge(rows_made, 5)
            pe.wait_ge(zeroed, 1)
            pe.wait_ge(zeroed_bank, 1)

            def scores(b, it, u):
                if u.first and u.j == 0:
                    pe.wait_ge(neg_in, rows_in(job_of(it, u) + 1))
                pe.wait_ge(exp_done, done(at(b, "exp", bank_used(b, "exp", u.n), it)))
                if u.kind == "attn":
                    k0 = it.keep(("heads", 0), lambda v: v % 2 * AQUERY_HALF, AQUERY_HALF)
                    q0, k0, at_byte = k0, k0 + 2 * GH * S, aqueries_u8
                    q0 = q0 + query_at(u.job * HG + u.j, u.col)
                else:
                    k0 = it.keep(("keys", 0), lambda v: node(v) % 2 * KEY_HALF, KEY_HALF)
                    q0 = it.keep(("queries", 0), lambda v: chunk(v) * QUERY_SLOT, QUERY_SLOT)
                    q0, at_byte = q0 + query_at(HG * u.job + u.j, u.col), queries_u8
                head = u.j if u.kind == "attn" else HG * u.job + u.j
                nc.tensor.matmul(ps_s[:, u.n % NSB, u.col:CH], operand(keys_u8, ROWS, k0 + key_at(head, u.kb * P), P),
                                 operand(at_byte, ROWS, q0, CH - u.col), start=True, stop=True).then_inc(qk_done, 1)

            def max_scores(b, it, u):
                if u.job == 0 and u.t == 0 and u.j == 0 and u.piece == 0:
                    if u.kind == "attn":
                        pe.wait_ge(heads_in, (it.v + u.ahead + 1) * (DMA * 2 * len(AQPARTS)))
                    else:
                        pe.wait_ge(parts_in, loaded(at(b, "split", int(has(b, "K2") and not b.flags.get("vlate")), it),
                                                    len(QPARTS)))
                pe.wait_ge(max_done, done(at(b, "max", bank_used(b, "max", u.n), it)))
                head = u.j if u.kind == "attn" else HG * u.job + u.j
                if u.kind == "attn":
                    k0 = it.keep(("heads", u.ahead), lambda v: (v + u.ahead) % 2 * AQUERY_HALF, AQUERY_HALF)
                    q0, k0, at_byte = k0 + query_at(u.job * HG + u.j, u.t * P), k0 + 2 * GH * S, aqueries_u8
                else:
                    v0 = -it.v if b.kind == "attn" else 0
                    q0 = it.keep(("queries", u.ahead), lambda v: chunk(v + v0 + u.ahead) * QUERY_SLOT, QUERY_SLOT)
                    k0 = it.keep(("keys", u.ahead), lambda v: node(v + v0 + u.ahead) % 2 * KEY_HALF, KEY_HALF)
                    q0, at_byte = q0 + query_at(head, u.t * P), queries_u8
                nc.tensor.matmul(ps_m[:, u.n % NSB, 0:u.w], operand(at_byte, KROWS, q0, P),
                                 operand(keys_u8, KROWS, k0 + key_at(head, u.k0), u.w),
                                 start=True, stop=True).then_inc(s1_done, 1)

            def pv(b, it, u):
                if u.first and u.j == 0:
                    pe.wait_ge(o_done, done(job_of(it, u)))
                    if u.kind == "attn":
                        pe.wait_ge(attn_v_in, (it.v + 1) * DMA)
                    else:
                        pe.wait_ge(graph_v_in[u.job], (it.v + 1) * DMA)
                if u.kind == "attn" and u.kb == KB - TPC and u.j == 0:
                    pe.wait_ge(attn_v_rest_in, (it.v + 1) * DMA)
                if b.flags.get("vlate") and u.n >= 0 and u.kb == KB - TPC and u.j == 0:
                    pe.wait_ge(late_v_in, DMA)
                pe.wait_ge(exp_done, done(at(b, "exp", u.n + 1, it)))
                size = (AD if u.kind == "attn" else GD) + 1
                live = 0 if u.kind == "attn" else u.job
                v0 = (u.kb * HG + u.j) * size
                nc.tensor.matmul(ps_o[32 * u.j:32 * u.j + size, u.col:CH], vlive[:, live, v0:v0 + size],
                                 probs[:, (u.n % NPS) * CH + u.col:(u.n % NPS + 1) * CH],
                                 start=u.first, stop=u.last).then_inc(pv_done, 1)

            def stage(b, it, st):
                if b.base["misc"] + st.n > 0:
                    pe.wait_ge(misc_free, at(b, "misc", st.n, it))
                if st.name == "M":
                    pe.wait_ge(neg_split, at(b, "M", st.k + 1, it))
                    nc.tensor.sem_inc(seen, 1)
                    last = nc.tensor.transpose(ps_x[0:MROWS * HG * TPC, 0:P // 2].bitcast(BF16),
                                               neg_parts[:, :, :].rearrange("p m c -> p (m c)"), ident_b[:])
                elif st.name == "O":
                    pe.wait_ge(o_done, done(at(b, "O", st.k + 1, it)))
                    slot = st.args[1] % 2
                    for t in range(TPC):
                        last = nc.tensor.transpose(ps_x[:, t * P:(t + 1) * P], o_sb[:, slot, t * P:(t + 1) * P],
                                                   ident[:])
                elif st.name == "E":
                    for t in range(TPC):
                        last = nc.tensor.transpose(ps_x[:, t * P:(t + 1) * P], n_t[:, t * P:(t + 1) * P], ident[:])
                elif st.name in ("OT", "Y1"):
                    if st.name == "Y1":
                        pe.wait_ge(y_in, (it.v + 3) * DMA)
                    for t in range(TPC):
                        src = o_tok[:, t * D:(t + 1) * D] if st.name == "OT" else y_now[:, t * D:(t + 1) * D]
                        last = nc.tensor.transpose(ps_x[:, t * P:(t + 1) * P], src, ident[:])
                elif st.name in ("Y2", "V2"):
                    stationary, w = (y_t, w_p) if st.name == "Y2" else (edge[:], w_kv[:, 3 * D:4 * D])
                    for t in range(TPC):
                        last = nc.tensor.matmul(ps_x[:, t * D:(t + 1) * D], stationary[:, t * P:(t + 1) * P], w,
                                                start=True, stop=True)
                else:
                    if st.name == "K1":
                        pe.wait_ge(xk_in, at(b, "K1", 1, it) * DMA)
                        loads = 1 if b.kind == "attn" else at(b, "K1", 1, it) - (NCH - 1)
                        pe.wait_ge(wkv_in, loads * DMA)
                        w, moving = w_kv[:, 0:D], xk[:]
                    elif st.name == "K2":
                        w, moving = w_kv[:, D:2 * D], edge[:]
                    elif st.name == "V1":
                        if b.kind != "attn" and not st.args:
                            pe.wait_ge(v_in, (at(b, "V1", st.k + 1, it) - 2 * NCH) * DMA)
                        w, moving = w_kv[:, 2 * D:3 * D], (xk[:] if b.kind == "attn" else n_t if st.args else xv)
                    elif st.name == "Q1":
                        loads = 1 if b.kind == "attn" else at(b, "query", 1, it) - (NCH - 1)
                        pe.wait_ge(wq_in, loads * DMA)
                        w, moving = w_q[:, 0:D], (xk[:] if b.kind == "attn" else n_t)
                    elif st.name == "Q2":
                        w, moving = w_q[:, D:2 * D], eq[:, bass.ds(q_slot(b, it) * CH, CH)]
                    elif st.name == "WO":
                        pe.wait_ge(wo_in, at(b, "WO", 1, it) * DMA)
                        w, moving = w_o, o_t
                    last = nc.tensor.matmul(ps_x[:], w, moving, start=True, stop=True)
                last.then_inc(misc_full, 1)

            for b in bodies:
                with each(pe, b) as it:
                    for st in b.steps:
                        cut = [len(st.max) * j // HG for j in range(HG + 1)]
                        for j in range(HG):
                            for u in st.exp[j:j + 1]:
                                scores(b, it, u)
                            for u in st.max[cut[j]:cut[j + 1]]:
                                max_scores(b, it, u)
                        for u in st.pv:
                            pv(b, it, u)
                        for x_ in st.stages:
                            stage(b, it, x_)

        @block.scalar
        def _(act):
            nc.scalar.sem_inc(exp_done, 1)
            nc.scalar.sem_inc(o_done, 1)
            act.wait_ge(ln, 6)
            nc.scalar.activation(stat[:, 3, :], stat[:, 2, :], ACT.Sqrt).then_inc(ln, 1)
            for c in range(NCH):
                act.wait_ge(xt_full, c + 1)
                bank = ps_s[:, c, :] if c < NSB else ps_m[:, 0, :]
                nc.scalar.activation(x_t[:, c * CH:(c + 1) * CH], bank, ACT.Copy).then_inc(xt_done, 1)
            act.wait_ge(ewb_done, 2)
            for n in range(2 * NCH):
                r, c = divmod(n, NCH)
                act.wait_ge(proj_full, n + 1)
                for dst in (a_whole[r], a_parts[r]):
                    last = nc.scalar.activation(dst[:, c * CH:(c + 1) * CH], ps_s[:, n % NSB, :], ACT.Identity,
                                                scale=(A_SCALE, 1.0)[r], bias=ba_col[:, (2, 1)[r]:(3, 2)[r]])
                last.then_inc(proj_free, 1)

            def exponentials(b, it, u):
                if u.near:
                    act.wait_ge(bias_done, done(at(b, "near", u.near_n + 1, it)))
                else:
                    act.wait_ge(qk_done, at(b, "exp", u.n + 1, it))
                act.wait_ge(pv_done, done(at(b, "exp", u.n, it)))
                nc.scalar.activation(probs[:, (u.n % NPS) * CH + u.col:(u.n % NPS + 1) * CH],
                                     ps_s[:, u.n % NSB, u.col:CH], ACT.Exp,
                                     scale=1.0 if u.kind == "attn" else G_SCALE).then_inc(exp_done, 1)

            def copy_outputs(b, it, u):
                act.wait_ge(pv_done, at(b, "exp", u.n + 1, it) + NPS)
                act.wait_ge(den_done, done(job_of(it, u)))
                nc.scalar.activation(o_sb[:, u.job % 2, :], ps_o[:], ACT.Copy).then_inc(o_done, 1)

            def stage(b, it, st):
                if st.name in ("O", "WO", "Y2"):
                    return
                if st.name in ("K2", "Q2"):
                    act.wait_ge(split_done, done(at(b, "split", st.k, it)))
                    act.wait_ge(parts_out, loaded(at(b, "split", st.k, it)))
                if st.name == "V2":
                    act.wait_ge(v_out, loaded(at(b, "V2", st.k, it)))
                if st.name == "M" and b.base["M"] + st.k > 0:
                    act.wait_ge(neg_in, rows_in(at(b, "M", st.k, it)))
                act.wait_ge(misc_full, at(b, "misc", st.n + 1, it))
                if st.name in ("K1", "V1", "Q1"):
                    e = 3 * (q_node(b, it) if st.name == "Q1" else kv_node(b, it, st)) + "QKV".index(st.name[0])
                    dst = {"K1": edge[:], "V1": edge[:], "Q1": eq[:, bass.ds(q_slot(b, it) * CH, CH)]}[st.name]
                    last = nc.scalar.activation(dst, ps_x[:], ACT.Identity, scale=ew_all[:, bass.ds(e, 1)],
                                                bias=ewb_all[:, bass.ds(e, 1)])
                elif st.name in ("K2", "Q2"):
                    nc.scalar.activation(whole[:], ps_x[:], ACT.Copy)
                    last = nc.scalar.activation(parts[:, 0, :], ps_x[:], ACT.Copy)
                elif st.name == "V2":
                    for g in range(2):
                        dst = v_new[:, g, :].rearrange("p (t j e) -> p t j e", t=TPC, j=HG)[:, :, :, 0:GD]
                        src = ps_x[:].rearrange("p (t g j e) -> p g t j e", g=2, j=HG, e=GD)[:, g]
                        last = nc.scalar.activation(dst, src, ACT.Copy)
                elif st.name == "M":
                    last = nc.scalar.activation(neg_rows[:], ps_x[0:MROWS * HG * TPC, 0:P // 2].bitcast(BF16), ACT.Copy)
                else:
                    dst = {"OT": o_t, "Y1": y_t}[st.name] if st.name != "E" else \
                        n_tok[:, bass.ds(chunk(it.v - 1) * CH, CH)]
                    last = nc.scalar.activation(dst, ps_x[:], ACT.Copy)
                last.then_inc(misc_free, 1)

            def copies(b, it, st):
                if st.pv and st.pv[-1].last:
                    copy_outputs(b, it, st.pv[-1])
                for x_ in st.stages:
                    stage(b, it, x_)
                if ("root", 0, NCH - 1) in st.ending:
                    root_of_output(0, NCH - 1)
                if ("silu", 0, NCH - 1) in st.ending:
                    exponential_of_output(0, NCH - 1)

            def root_of_output(c0, c1):
                act.wait_ge(end_chain, 6 + (END_LINKS if c0 else 0))
                nc.scalar.activation(stat[:, 3, TPC * c0:TPC * c1], stat[:, 2, TPC * c0:TPC * c1], ACT.Sqrt)\
                    .then_inc(end_chain, 1)

            def exponential_of_output(c0, c1):
                act.wait_ge(end_chain, NORM_LINKS + (END_LINKS if c0 else 0))
                nc.scalar.activation(sq_tok[:, c0 * CH:c1 * CH], n_tok[:, c0 * CH:c1 * CH], ACT.Exp, scale=-1.0)\
                    .then_inc(end_chain, 1)

            for b in bodies:
                with each(act, b) as it:
                    before = None
                    for st in b.steps:
                        for u in st.exp[:2]:
                            exponentials(b, it, u)
                        if before:
                            copies(b, it, before)
                        for u in st.exp[2:]:
                            exponentials(b, it, u)
                        before = st
                        if not st.exp:
                            copies(b, it, st)
                            before = None
                    if before:
                        copies(b, it, before)

            root_of_output(NCH - 1, NCH)
            exponential_of_output(NCH - 1, NCH)

        @block.vector
        def _(dve):
            tiles = lambda ap: ap.rearrange("p (t d) -> p t d", d=D)
            per_tile = lambda ap: ap.unsqueeze(2).to_broadcast([P, KB, D])
            nc.vector.sem_inc(max_done, 1)
            nc.vector.sem_inc(bias_done, 1)
            nc.vector.sem_inc(den_done, 2)
            dve.wait_ge(x_in, DMA)
            nc.vector.reduce_sum(stat[:, 0, :], tiles(x_tok), axis=AX_X).then_inc(ln, 1)
            dve.wait_ge(ln, 1)
            nc.vector.tensor_scalar(stat[:, 1, :], stat[:, 0, :], 1.0 / D, None, ALU.mult).then_inc(ln, 1)
            dve.wait_ge(ln, 2)
            nc.vector.tensor_tensor(tiles(x_tok), tiles(x_tok), per_tile(stat[:, 1, :]), ALU.subtract).then_inc(ln, 1)
            dve.wait_ge(ln, 3)
            nc.vector.tensor_tensor(x_t, x_tok, x_tok, ALU.mult).then_inc(ln, 1)
            dve.wait_ge(ln, 4)
            nc.vector.reduce_sum(stat[:, 0, :], tiles(x_t), axis=AX_X).then_inc(ln, 1)
            dve.wait_ge(ln, 5)
            nc.vector.tensor_scalar(stat[:, 2, :], stat[:, 0, :], 1.0 / D, LN_EPS, ALU.mult, ALU.add).then_inc(ln, 1)
            dve.wait_ge(ln, 7)
            nc.vector.reciprocal(stat[:, 0, :], stat[:, 3, :]).then_inc(ln, 1)
            dve.wait_ge(ln, 8)
            nc.vector.tensor_tensor(tiles(x_tok), tiles(x_tok), per_tile(stat[:, 0, :]), ALU.mult).then_inc(ln, 1)
            dve.wait_ge(small_in, 4 * DMA)
            nc.vector.tensor_tensor(ewb_all[:], ewb_all[:], ew_all[:], ALU.mult).then_inc(ewb_done, 1)
            nc.vector.tensor_scalar(ba_col[:, 2:3], ba_col[:, 0:1], A_SCALE, None, ALU.mult).then_inc(ewb_done, 1)
            nc.vector.memset(line_sb[:, 0:P], MASKED)
            nc.vector.memset(line_sb[:, NEAR + P + NEAR + 1:2 * (NEAR + P)], MASKED)
            dve.wait_ge(line_full, 1)
            nc.vector.tensor_copy(line_sb[:, P:NEAR + P], ps_m[0:AH, 1, P:NEAR + P]).then_inc(line_done, 1)
            dve.wait_ge(line_full, 2)
            nc.vector.tensor_copy(line_sb[:, NEAR + P:NEAR + P + NEAR + 1], ps_m[0:AH, 2, 0:NEAR + 1]).then_inc(line_done, 1)
            nc.vector.memset(ps_o[:], 0.0).then_inc(zeroed_bank, 1)
            for r in range(2):
                part = lambda n: a_parts[r][:, n * S:(n + 1) * S]
                dve.wait_ge(proj_free, NCH * (r + 1))
                if r:
                    dve.wait_ge(aparts_done, 3)
                nc.vector.tensor_tensor(a_rest, a_whole[r], part(0), ALU.subtract).then_inc(aparts_done, 1)
                dve.wait_ge(aparts_done, 3 * r + 1)
                nc.vector.tensor_copy(part(1), a_rest).then_inc(aparts_done, 1)
                dve.wait_ge(aparts_done, 3 * r + 2)
                nc.vector.tensor_tensor(part(2), a_rest, part(1), ALU.subtract).then_inc(aparts_done, 1)
            dve.wait_ge(rows_made, 1)
            for c in range(NCH):
                n = 2 * NCH + c
                dve.wait_ge(proj_full, n + 1)
                for g in range(AH // HG):
                    grp = lambda ap: ap.rearrange("p (k g j e) -> p g k j e", g=AH // HG, j=HG, e=AD)[:, g]
                    dst = va_sb.rearrange("p (g k j e) -> p g k j e", g=AH // HG, k=KB, j=HG)[
                        :, g, TPC * c:TPC * (c + 1), :, 0:AD]
                    bias = bv_all.rearrange("p (g j e) -> p g j e", g=AH // HG, j=HG)[:, g].unsqueeze(1).to_broadcast(
                        [P, TPC, HG, AD])
                    last = nc.vector.tensor_tensor(dst, grp(ps_s[:, n % NSB, :]), bias, ALU.add)
                last.then_inc(proj_free, 1)

            def add_bias(b, it, u):
                half = int(u.n >= 4 * (ASTEPS // 2))
                if u.j == 0:
                    dve.wait_ge(bias_kq_in[half], (it.v + 1) * DMA)
                dve.wait_ge(qk_done, at(b, "exp", u.n + 1, it))
                near = ps_s[:, u.n % NSB, u.col:u.col + u.near]
                nc.vector.tensor_tensor(near, near, bias_kq[:, half, u.j, u.band:u.band + u.near],
                                        ALU.add).then_inc(bias_done, 1)

            def maxima(b, it, u):
                if u.near and u.j == 0:
                    dve.wait_ge(bias_qk_in[u.half], (it.v + (u.ahead + 1)) * DMA)
                dve.wait_ge(s1_done, at(b, "max", u.n + 1, it))
                if u.near:
                    nc.vector.sem_inc(seen, 1)
                src, dst = ps_m[:, u.n % NSB, 0:u.w], mx[:, u.job % 2, u.t, u.j, u.piece:u.piece + 1]
                if u.near:
                    nc.vector.tensor_tensor_reduce(out=src, in0=src, in1=bias_qk[:, u.half, u.j, NEAR - u.w:NEAR],
                                                   scale=1.0, scalar=-3.0e38, op0=ALU.add, op1=ALU.max,
                                                   accum_out=dst).then_inc(max_done, 1)
                else:
                    nc.vector.reduce_max(dst, src, axis=AX_X).then_inc(max_done, 1)

            def negate(b, it, st):
                kind, _, job = st.fin
                dve.wait_ge(max_done, done(at(b, "max", st.max[-1].n + 1, it)))
                if b.base["m"] + st.fin_n > 0:
                    dve.wait_ge(neg_split, at(b, "m", st.fin_n, it))
                dst = neg_max[:].rearrange("p (j t) -> p t j", j=HG)
                if kind == "graph":
                    last = nc.vector.tensor_reduce(dst, mx[:, job % 2, :, :, 0:S // CH], op=ALU.max, axis=AX_X, negate=True)
                else:
                    for t in range(TPC):
                        n = max(x_["pieces"] for u_ in A_MAX for x_ in u_ if x_["job"] == job and x_["t"] == t)
                        last = nc.vector.tensor_reduce(dst[:, t, :], mx[:, job % 2, t, :, 0:n], op=ALU.max, axis=AX_X, negate=True)
                last.then_inc(neg_done, 1)

            def stage(b, it, st):
                if st.name not in ("O", "WO", "Y2"):
                    return
                dve.wait_ge(misc_full, at(b, "misc", st.n + 1, it))
                if st.name == "O":
                    size = AD if st.args[0] == "attn" else GD
                    o4 = ps_x[:].rearrange("p (t j e) -> p t j e", j=HG, e=32)
                    nc.vector.reciprocal(rden[:], o4[:, :, :, size]).then_inc(den_done, 1)
                    dve.wait_ge(den_done, at(b, "O", st.k + 1, it) + 2)
                    if st.args[0] == "attn":
                        dst = y_tok[:].rearrange("p (t f) -> p t f", f=D)[
                            :, TPC * st.args[1]:TPC * (st.args[1] + 1), bass.ds(it.v * (HG * AD), HG * AD)]
                    else:
                        dst = o_tok.rearrange("p (t f) -> p t f", f=D)[
                            :, :, HG * GD * st.args[1]:HG * GD * (st.args[1] + 1)]
                    last = nc.vector.tensor_tensor(dst.rearrange("p t (j e) -> p t j e", j=HG), o4[:, :, :, 0:size],
                                                   rden[:].unsqueeze(3).to_broadcast([P, TPC, HG, size]), ALU.mult)
                elif st.name == "WO":
                    dve.wait_ge(n_out, loaded(STORED if b.flags["tokens"] else at(b, "WO", st.k, it)))
                    last = nc.vector.scalar_tensor_tensor(
                        out=n_t, in0=ps_x[:], scalar=act_all[:, bass.ds(node(it.v - 1), 1)],
                        in1=eq[:, bass.ds(chunk(it.v - 1) * CH, CH)], op0=ALU.mult, op1=ALU.add)
                else:
                    last = nc.vector.tensor_tensor(s_tok[:, bass.ds(it.v * CH, CH)].rearrange("p (t d) -> p t d", d=D),
                                                   ps_x[:].rearrange("p (t d) -> p t d", d=D),
                                                   bp_all.unsqueeze(1).to_broadcast([P, TPC, D]), ALU.add)
                last.then_inc(misc_free, 1)

            def small(b, it, st):
                if st.fin:
                    negate(b, it, st)
                for x_ in st.stages:
                    stage(b, it, x_)
                for name, c0, c1 in st.ending:
                    if name == "norm":
                        e = [y for z in b.steps for y in z.stages if y.name == "E"][0]
                        dve.wait_ge(misc_free, at(b, "misc", e.n + 1, it))
                        norm_output(c0, c1)
                    elif name == "output":
                        output(c0, c1)

            def link(ins, n):
                ins.then_inc(end_chain, 1)
                dve.wait_ge(end_chain, n)

            def norm_output(c0, c1):
                n = END_LINKS if c0 else 0
                tok = tiles(n_tok)[:, TPC * c0:TPC * c1, :]
                sq = tiles(sq_tok)[:, TPC * c0:TPC * c1, :]
                col = lambda k: stat[:, k, TPC * c0:TPC * c1]
                spread = lambda ap: ap.unsqueeze(2).to_broadcast([P, TPC * (c1 - c0), D])
                row = lambda ap: ap.unsqueeze(1).to_broadcast([P, TPC * (c1 - c0), D])
                link(nc.vector.reduce_sum(col(0), tok, axis=AX_X), n + 1)
                link(nc.vector.tensor_scalar(col(1), col(0), 1.0 / D, None, ALU.mult), n + 2)
                link(nc.vector.tensor_tensor(tok, tok, spread(col(1)), ALU.subtract), n + 3)
                link(nc.vector.tensor_tensor(sq, tok, tok, ALU.mult), n + 4)
                link(nc.vector.reduce_sum(col(0), sq, axis=AX_X), n + 5)
                link(nc.vector.tensor_scalar(col(2), col(0), 1.0 / D, FFN_EPS, ALU.mult, ALU.add), n + 6)
                dve.wait_ge(end_chain, n + 7)
                link(nc.vector.reciprocal(col(1), col(3)), n + 8)
                link(nc.vector.tensor_tensor(tok, tok, spread(col(1)), ALU.mult), n + 9)
                if not c0:
                    dve.wait_ge(end_in, 3 * DMA)
                link(nc.vector.tensor_tensor(tok, tok, row(g_all), ALU.mult), n + 10)
                nc.vector.tensor_tensor(tok, tok, row(b_all), ALU.add).then_inc(end_chain, 1)

            def output(c0, c1):
                n = NORM_LINKS + 1 + (END_LINKS if c0 else 0)
                at_ = lambda ap: ap[:, c0 * CH:c1 * CH]
                dve.wait_ge(end_chain, n)
                link(nc.vector.tensor_scalar(at_(sq_tok), at_(sq_tok), 1.0, None, ALU.add), n + 1)
                link(nc.vector.reciprocal(at_(sq_tok), at_(sq_tok)), n + 2)
                link(nc.vector.tensor_tensor(at_(n_tok), at_(n_tok), at_(sq_tok), ALU.mult), n + 3)
                link(nc.vector.tensor_tensor(at_(n_tok), at_(n_tok), at_(s_tok), ALU.mult), n + 4)
                nc.vector.tensor_tensor(at_(n_tok), at_(n_tok), at_(x_end), ALU.add).then_inc(end_chain, 1)

            for b in bodies:
                with each(dve, b) as it:
                    before = None
                    for st in b.steps:
                        cut = [len(st.max) * j // HG for j in range(HG + 1)]
                        for j in range(HG):
                            for u in st.exp[j:j + 1]:
                                if u.near:
                                    add_bias(b, it, u)
                            for u in st.max[cut[j]:cut[j + 1]]:
                                maxima(b, it, u)
                            if j == 1 and before:
                                small(b, it, before)
                        before = st
                        if not st.max:
                            small(b, it, st)
                            before = None
                    if before:
                        small(b, it, before)

            dve.wait_ge(misc_free, total["misc"])
            norm_output(NCH - 1, NCH)
            output(NCH - 1, NCH)

        @block.gpsimd
        def _(pool):
            nc.gpsimd.sem_inc(split_done, 1)
            for n, m in enumerate((ident, ident_b)):
                nc.gpsimd.memset(m[:], 0.0).then_inc(pool_chain, 1)
                pool.wait_ge(pool_chain, n + 1)
                nc.gpsimd.affine_select(out=m[:], in_=m[:], compare_op=ALU.not_equal, fill=1.0, base=0,
                                        pattern=[[-1, P]], channel_multiplier=1).then_inc(ident_made, 1)
            ones2 = 0x3F803F80
            half = lambda r0, r1, par: keys[r0:r1, par * GH * S:(par + 1) * GH * S].bitcast(mybir.dt.uint32)
            pool.wait_ge(ident_made, 2)
            nc.gpsimd.memset(va_sb, 1.0).then_inc(rows_made, 1)
            pool.wait_ge(rows_made, 1)
            nc.gpsimd.memset(v_new[:, :, :], 1.0).then_inc(rows_made, 1)
            pool.wait_ge(rows_made, 2)
            nc.gpsimd.memset(half(64, KROWS, 1), 0).then_inc(rows_made, 1)
            pool.wait_ge(rows_made, 3)
            nc.gpsimd.memset(half(KROWS, ROWS, 1), ones2).then_inc(rows_made, 1)
            pool.wait_ge(rows_made, 4)
            nc.gpsimd.memset(aqueries[64:KROWS, :].bitcast(mybir.dt.uint32), 0).then_inc(zeroed, 1)
            pool.wait_ge(zeroed, 1)
            pool.wait_ge(va_out, DMA)
            pool.wait_ge(aparts_out, 2 * DMA)
            nc.gpsimd.memset(half(KROWS, ROWS, 0), ones2).then_inc(rows_made, 1)

            def chain(b, it, fins, splits, k):
                return 3 * at(b, "m", fins, it) + 2 * at(b, "split", splits, it) + (k + 2)

            def split_maxima(b, it, n, splits):
                pool.wait_ge(neg_done, at(b, "m", n + 1, it))
                if b.base["m"] + n > 0:
                    pool.wait_ge(neg_in, rows_in(at(b, "m", n, it)))
                nc.gpsimd.sem_inc(seen, 1)
                nc.gpsimd.tensor_copy(neg_parts[:, 0, :], neg_max[:]).then_inc(pool_chain, 1)
                pool.wait_ge(pool_chain, chain(b, it, n, splits, 1))
                nc.gpsimd.tensor_tensor(neg_rest[:], neg_max[:], neg_parts[:, 0, :], ALU.subtract).then_inc(pool_chain, 1)
                pool.wait_ge(pool_chain, chain(b, it, n, splits, 2))
                nc.gpsimd.sem_inc(seen, 1)
                nc.gpsimd.tensor_copy(neg_parts[:, 1, :], neg_rest[:]).then_inc(pool_chain, 1)
                pool.wait_ge(pool_chain, chain(b, it, n, splits, 3))
                nc.gpsimd.tensor_tensor(neg_parts[:, 2, :], neg_rest[:], neg_parts[:, 1, :], ALU.subtract)\
                    .then_inc(neg_split, 1)

            def split(b, it, st, fins):
                pool.wait_ge(misc_free, at(b, "misc", st.n + 1, it))
                nc.gpsimd.tensor_tensor(rest[:], whole[:], parts[:, 0, :], ALU.subtract).then_inc(pool_chain, 1)
                pool.wait_ge(pool_chain, chain(b, it, fins, st.k, 1))
                nc.gpsimd.sem_inc(seen, 1)
                nc.gpsimd.tensor_copy(parts[:, 1, :], rest[:]).then_inc(pool_chain, 1)
                pool.wait_ge(pool_chain, chain(b, it, fins, st.k, 2))
                nc.gpsimd.tensor_tensor(parts[:, 2, :], rest[:], parts[:, 1, :], ALU.subtract).then_inc(split_done, 1)

            for b in bodies:
                if not any(st.fin or x_.name in ("K2", "Q2") for st in b.steps for x_ in (st.stages or [Stage("", (), 0)])):
                    continue
                with each(pool, b) as it:
                    fins = splits = 0
                    for st in b.steps:
                        if st.fin:
                            split_maxima(b, it, fins, splits)
                            fins += 1
                        for x_ in st.stages:
                            if x_.name in ("K2", "Q2"):
                                split(b, it, x_, fins)
                                splits += 1

        @block.sync
        def _(sp):
            for s in (parts_in, parts_out, v_out, n_out):
                nc.sync.sem_inc(s, 1)
            sp.dma_start(x_tok.rearrange("p (t d) -> p t d", d=D), x.rearrange("(t p) d -> p t d", p=P)).then_inc(x_in, DMA)
            sp.dma_start(hot_sb, hot).then_inc(hot_in, DMA)
            sp.dma_start(rel_sb, rel).then_inc(hot_in, DMA)
            sp.dma_start(wa_sb, wa).then_inc(wa_in, DMA)
            sp.dma_start(bv_all, ba[2 * D:3 * D].unsqueeze(0).to_broadcast([P, D])).then_inc(wa_in, DMA)
            sp.dma_start(ew_all[:], ew.unsqueeze(0).to_broadcast([P, 3 * NODES])).then_inc(small_in, DMA)
            sp.dma_start(ewb_all[:], be).then_inc(small_in, DMA)
            sp.dma_start(act_all[:], act_w.unsqueeze(0).to_broadcast([P, NODES])).then_inc(small_in, DMA)
            sp.dma_start(ba_col[:, 0:2], ba_qk).then_inc(small_in, DMA)
            sp.dma_start(w_kv[:], wkv[0]).then_inc(wkv_in, DMA)
            sp.dma_start(w_q[:], wq[0]).then_inc(wq_in, DMA)
            sp.wait_ge(xt_done, NCH)
            sp.dma_start(acts_d[0], x_t).then_inc(xt_out, DMA)
            sp.wait_ge(line_done, 2)
            sp.dma_start(line_d, line_sb.rearrange("h (r n) -> h r n", r=2)).then_inc(line_out, DMA)
            sp.wait_ge(line_out, DMA)
            line_len = NEAR + P
            for r in range(2):
                src = bass.AP(tensor=line_d.tensor, offset=r * line_len + P,
                              ap=[[2 * line_len, AH], [-1, P], [1, NEAR]])
                sp.dma_start(band_d[r], src).then_inc(band_out, DMA)
            for r in range(2):
                sp.wait_ge(aparts_done, 3 * (r + 1))
                sp.dma_start(parts_d[r].rearrange("n p s -> p n s"), a_parts[r].rearrange("p (n s) -> p n s", n=3))\
                    .then_inc(aparts_out, DMA)
            sp.wait_ge(proj_free, 3 * NCH)
            sp.dma_start(va_d.rearrange("g p e -> p g e"), va_sb.rearrange("p (g e) -> p g e", g=AH // HG))\
                .then_inc(va_out, DMA)
            sp.wait_ge(xt_out, DMA)
            sp.wait_ge(aparts_out, 2 * DMA)
            sp.wait_ge(zeroed, 1)
            sp.wait_ge(rows_made, 4)
            keys4 = keys[:].rearrange("p (a h s) -> p a h s", a=2, h=GH)
            queries4 = queries[:].rearrange("p (c h s) -> p c h s", c=NCH, h=GH)

            def heads(hg, part=None):
                rows = [(side, t) for side in range(2) for t in range(len(AQPARTS))]
                for side, t in rows if part is None else rows[part::HEAD_LOADS]:
                    src = parts_d[side, (AQPARTS, AKPARTS)[side][t], bass.ds(hg * (HG * AD), HG * AD), :]
                    to = slice(AD * t, AD * (t + 1))
                    if side == 0:
                        d = aqueries[to, bass.ds((hg % 2) * (HG * S), HG * S)]
                        src, d = src.rearrange("(j d) (i q) -> d i j q", d=AD, q=CH), \
                            d.rearrange("d (i j q) -> d i j q", i=NCH, j=HG)
                    else:
                        d = keys[to, bass.ds((hg % 2) * (HG * S) + GH * S, HG * S)]
                        src, d = src.rearrange("(j d) s -> d j s", d=AD), d.rearrange("d (j s) -> d j s", j=HG)
                    sp.dma_start(d, src).then_inc(heads_in, DMA)

            def bias(side, hg, half_):
                dst, s = ((bias_kq, bias_kq_in), (bias_qk, bias_qk_in))[side]
                sp.dma_start(dst[:, half_], band_d[side, bass.ds(hg * HG, HG)].rearrange("h p n -> p h n"))\
                    .then_inc(s[half_], DMA)

            def attention_values(hg, c0, c1, s):
                part = slice(c0 * A_CHUNK, c1 * A_CHUNK)
                sp.dma_start(vlive[:, 0, part], va_d[bass.ds(hg, 1), :, part].rearrange("g p e -> (g p) e")).then_inc(s, DMA)

            sp.wait_ge(va_out, DMA)
            sp.wait_ge(band_out, 2 * DMA)
            bias(1, 0, 0)
            bias(1, 0, 1)
            heads(0)
            attention_values(0, 0, NCH - 1, attn_v_in)
            bias(0, 0, 0)

            def key_inputs(it):
                n = node(it.v) + 1
                sp.dma_start(xk[:], acts_d[bass.ds(n // 5, 1), :, bass.ds(chunk(it.v) * CH, CH)]
                             .rearrange("a p s -> (a p) s")).then_inc(xk_in, DMA)
                sp.dma_start(w_kv[:], wkv[bass.ds(n, 1)].rearrange("a p e -> (a p) e")).then_inc(wkv_in, DMA)

            def load(b, it, s, what):
                if what == "attn_v_rest":
                    sp.wait_ge(pv_done, at(b, "exp", 0, it) + NPS)
                    attention_values(it.v, NCH - 1, NCH, attn_v_rest_in)
                elif what == "attn_v_next":
                    used = 4 * (ASTEPS - TPC)
                    sp.wait_ge(pv_done, at(b, "exp", used, it) + NPS)
                    attention_values(it.v + 1, 0, NCH - 1, attn_v_in)
                elif what in ("graph_v0", "graph_v1"):
                    g = int(what[-1])
                    lag = 4 if b.flags["after"] and g == 0 else 0
                    sp.wait_ge(pv_done, at(b, "exp", 0, it) + (NPS - lag))
                    sp.wait_ge(v_out, loaded(at(b, "V2", 0, it)))
                    w = V_CHUNK * (NCH - 1 if b.flags["vlate"] else NCH)
                    sp.dma_start(vlive[:, g, 0:w], vg_d[bass.ds(node(it.v) % 2, 1), g, :, 0:w].rearrange("a p e -> (a p) e"))\
                        .then_inc(graph_v_in[g], DMA)
                elif what == "late_v":
                    sp.wait_ge(v_out, loaded(at(b, "V2", 1, it)))
                    sp.wait_ge(pv_done, at(b, "exp", 0, it) + NPS)
                    sp.dma_start(vlive[:, :, (NCH - 1) * V_CHUNK:NCH * V_CHUNK],
                                 vg_d[1, :, :, (NCH - 1) * V_CHUNK:NCH * V_CHUNK].rearrange("g p e -> p g e"))\
                        .then_inc(late_v_in, DMA)
                elif what == "node_in":
                    sp.wait_ge(misc_full, at(b, "misc", 0, it))
                    if b.kind == "attn":
                        sp.dma_start(xk[:], acts_d[0, :, bass.ds(it.v * CH, CH)]).then_inc(xk_in, DMA)
                    elif b.flags["kprep"] and not b.flags["vlate"]:
                        key_inputs(it)
                    if b.kind != "attn" and b.flags["after"]:
                        sp.dma_start(w_o, wo[bass.ds(node(it.v - 1), 1)].rearrange("a p e -> (a p) e")).then_inc(wo_in, DMA)
                    if b.kind != "attn" and b.flags["nextq"]:
                        sp.dma_start(w_q[:], wq[bass.ds(node(it.v - 1) + 1, 1)].rearrange("a p e -> (a p) e"))\
                            .then_inc(wq_in, DMA)
                    if has(b, "Y1"):
                        sp.wait_ge(exp_done, done(at(b, "exp", 0, it)))
                        if b.it0 == 0:
                            sp.dma_start(w_p, wp).then_inc(y_in, DMA)
                            sp.dma_start(bp_all, bp.unsqueeze(0).to_broadcast([P, D])).then_inc(y_in, DMA)
                        sp.dma_start(y_now, y_tok[:, bass.ds(it.v * CH, CH)]).then_inc(y_in, DMA)
                elif what == "key_in":
                    v = [y for z in b.steps for y in z.stages if y.name == "V2"][0]
                    sp.wait_ge(misc_full, at(b, "misc", v.n + 1, it))
                    key_inputs(it)
                elif isinstance(what, tuple):
                    sp.wait_ge(exp_done, done(at(b, "exp", 0, it)))
                    heads(it.v + 1, what[1])
                elif what == "bias_b":
                    sp.wait_ge(bias_done, done(at(b, "near", 0, it)))
                    bias(0, it.v, 1)
                elif what == "bias_a":
                    used = sum(1 for st in b.steps for u in st.exp if u.near and u.n < 4 * (ASTEPS // 2))
                    sp.wait_ge(bias_done, done(at(b, "near", used, it)))
                    bias(0, it.v + 1, 0)
                elif what == "max_bias_a":
                    sp.wait_ge(max_done, done(at(b, "max", 0, it)))
                    bias(1, it.v + 1, 0)
                elif what == "max_bias_b":
                    used = sum(len(st.max) for st in b.steps[:s])
                    sp.wait_ge(max_done, done(at(b, "max", used, it)))
                    bias(1, it.v + 1, 1)
                elif what == "split":
                    x_ = [y for st in b.steps[:s + 1] for y in st.stages if y.name in ("K2", "Q2")][-1]
                    sp.wait_ge(split_done, done(at(b, "split", x_.k + 1, it)))
                    sp.wait_ge(parts_in, loaded(at(b, "split", x_.k, it), len(QPARTS)))
                    sp.dma_start(split_d.rearrange("n p s -> p n s"), parts[:, :, :]).then_inc(parts_out, DMA)
                    sp.wait_ge(parts_out, loaded(at(b, "split", x_.k + 1, it)))
                    sp.wait_ge(exp_done, done(at(b, "exp", 0, it)))
                    for t in range(len(QPARTS)):
                        rows = slice(GD * t, GD * (t + 1))
                        if x_.name == "K2":
                            n, c0 = kv_node(b, it) % 2, (it.v if b.kind == "attn" else chunk(it.v)) * CH
                            dst = keys4[rows, bass.ds(n, 1), :, bass.ds(c0, CH)]
                        else:
                            dst = queries4[rows, bass.ds(q_slot(b, it), 1), :, :]
                        src = split_d[(KPARTS if x_.name == "K2" else QPARTS)[t]].rearrange("(h d) s -> d h s", d=GD)
                        sp.dma_start(dst.rearrange("d a h s -> d (a h) s"), src).then_inc(parts_in, DMA)
                elif what == "v_in":
                    sp.wait_ge(misc_full, at(b, "misc", 0, it))
                    src = acts_d[bass.ds((node(it.v) + 2) // 2, 1), :, bass.ds(chunk(it.v) * CH, CH)].rearrange(
                        "a p s -> (a p) s")
                    sp.wait_ge(n_out, loaded(at(b, "WO", int(b.flags["after"]), it)))
                    sp.dma_start(xv, src).then_inc(v_in, DMA)
                elif what == "v_out":
                    x_ = [y for st in b.steps[:s + 1] for y in st.stages if y.name == "V2"][-1]
                    sp.wait_ge(misc_free, at(b, "misc", x_.n + 1, it))
                    c0 = it.v if b.kind == "attn" else chunk(it.v - 1) if x_.args else chunk(it.v)
                    dst = vg_d[bass.ds(kv_node(b, it, x_) % 2, 1), :, :, bass.ds(c0 * V_CHUNK, V_CHUNK)]
                    sp.dma_start(dst.rearrange("a g p e -> p (a g) e"), v_new[:, :, :]).then_inc(v_out, DMA)
                elif what == "end_in":
                    sp.wait_ge(exp_done, done(at(b, "exp", 0, it)))
                    sp.dma_start(x_end.rearrange("p (t d) -> p t d", d=D), x.rearrange("(t p) d -> p t d", p=P))\
                        .then_inc(end_in, DMA)
                    sp.dma_start(g_all, ln_g.unsqueeze(0).to_broadcast([P, D])).then_inc(end_in, DMA)
                    sp.dma_start(b_all, ln_b.unsqueeze(0).to_broadcast([P, D])).then_inc(end_in, DMA)
                elif what == "output":
                    store_output(0, NCH - 1)
                elif what == "n_out":
                    x_ = [y for st in b.steps[:s + 1] for y in st.stages if y.name == "WO"][-1]
                    sp.wait_ge(misc_free, at(b, "misc", x_.n + 1, it))
                    dst = acts_d[bass.ds(node(it.v - 1) + 1, 1), :, bass.ds(chunk(it.v - 1) * CH, CH)]
                    sp.dma_start(dst.rearrange("a p s -> (a p) s"), n_t).then_inc(n_out, DMA)

            def maximum_rows(b, it, x_):
                kind, ahead, job = x_.args
                sp.wait_ge(misc_free, at(b, "misc", x_.n + 1, it))
                n = HG * TPC
                for m in range(MROWS):
                    row = slice(KROWS + m, KROWS + m + 1)
                    if kind == "attn":
                        to = aqueries[row, bass.ds((it.v + ahead) % 2 * (HG * S) + job * (HG * CH), HG * CH)]
                    else:
                        to = queries[row, bass.ds(chunk(graph_it(b, it, ahead)) * (GH * CH) + job * (HG * CH), HG * CH)]
                    sp.dma_start(to, neg_rows[m * n:(m + 1) * n, :]).then_inc(neg_in, DMA)

            def store_output(c0, c1):
                sp.wait_ge(end_chain, END_LINKS * (2 if c0 else 1))
                by_token = lambda ap: ap.rearrange("p (t d) -> p t d", d=D)[:, TPC * c0:TPC * c1, :]
                sp.dma_start(out.rearrange("(t p) d -> p t d", p=P)[:, TPC * c0:TPC * c1, :], by_token(n_tok))\
                    .then_inc(end_out, DMA)

            for b in bodies:
                with each(sp, b, keep=False) as it:
                    for s, st in enumerate(b.steps):
                        for x_ in st.stages:
                            if x_.name == "M":
                                maximum_rows(b, it, x_)
                        for what in st.loads:
                            load(b, it, s, what)

            sp.wait_ge(n_out, loaded(STORED))
            store_output(NCH - 1, NCH)
            sp.wait_ge(end_out, 2 * DMA)


def bucket_one_hot():
    buckets, far = 32, 128
    exact = buckets // 2
    d = np.arange(NEAR + 1)
    log = np.log(d.astype(np.float32) / np.float32(exact) + np.float32(1e-10))
    large = exact + (log / np.float32(np.log(far / exact)) * np.float32(buckets - exact)).astype(np.int64)
    bucket = np.where(d < exact, d, np.minimum(large, buckets - 1))
    assert bucket[P] == buckets - 1
    hot = np.zeros((buckets, 2, NEAR + P), np.float32)
    for r in range(2):
        for i in range(NEAR + P):
            dist = i - P if r == 0 else NEAR - i
            if dist >= 0:
                hot[bucket[dist], r, i] += 1.0
                hot[buckets - 1, r, i] -= 1.0
    return hot.reshape(buckets, 2 * (NEAR + P))


def kernel(**inputs):
    import concourse.bacc as bacc
    from concourse.bass_utils import run_bass_kernel_spmd

    a = {k: np.asarray(v) for k, v in inputs.items()}
    q_edge, k_edge, v_edge, first = [], [], [], 0
    for c in range(NODES):
        n = min(c + 1, 5)
        q_edge.append(first + n - 1)
        k_edge.append(first)
        v_edge.append(first + n // 2)
        first += n
    we = a["L0_ffn_We"]
    side = lambda *ws: np.ascontiguousarray(np.concatenate(ws, axis=-1))
    edges = np.stack([q_edge, k_edge, v_edge], axis=1).reshape(-1)
    arrays = {
        "x": a["L0_attn_x"].reshape(S, D),
        "wa": np.ascontiguousarray(a["L0_attn_W_attn"].T),
        "ba": a["L0_attn_b_attn"],
        "ba_qk": np.ascontiguousarray(a["L0_attn_b_attn"].reshape(3, D)[:2].T),
        "wp": np.ascontiguousarray(a["L0_attn_W_proj"].T),
        "bp": a["L0_attn_b_proj"],
        "rel": a["L0_attn_rel_emb"],
        "hot": bucket_one_hot(),
        "wkv": side(we[k_edge], a["L0_ffn_Wk"], we[v_edge], a["L0_ffn_Wv"]),
        "wq": side(we[q_edge], a["L0_ffn_Wq"]),
        "wo": a["L0_ffn_Wo"],
        "be": np.ascontiguousarray(a["L0_ffn_be"][edges].T),
        "ew": a["L0_ffn_ew"].reshape(-1),
        "act_w": a["L0_ffn_act_w"],
        "ln_g": a["L0_ffn_ln_g"],
        "ln_b": a["L0_ffn_ln_b"],
    }
    nc = bacc.Bacc("TRN2", target_bir_lowering=False, num_devices=1)
    nc.disable_value_cache = True
    args = [nc.dram_tensor("in_" + k, v.shape, mybir.dt.from_np(v.dtype), kind="ExternalInput").ap()
            for k, v in arrays.items()]
    out = nc.dram_tensor("out", (S, D), F32, kind="ExternalOutput").ap()
    build(nc, *args, out)
    got = run_bass_kernel_spmd(nc, [{"in_" + k: v for k, v in arrays.items()}], core_ids=[0])
    return got.results[0]["out"].reshape(1, S, D)
```
